# Optimizing a Trainium2 kernel written in Bass

```python
import numpy as np
import jax
import jax.numpy as jnp

def _softmax(x, axis=-1):
    return jax.nn.softmax(x, axis=axis)

def _gelu(x):
    return jax.nn.gelu(x, approximate=True)

def _silu(x):
    return jax.nn.silu(x)

def _sigmoid(x):
    return jax.nn.sigmoid(x)

def _layernorm(x, axis=-1, eps=1e-05):
    m = jnp.mean(x, axis=axis, keepdims=True)
    v = jnp.var(x, axis=axis, keepdims=True)
    return (x - m) / jnp.sqrt(v + eps)

def _scatter_add(tgt, idx, src, axis=0):
    return tgt.at[idx].add(src)

def _segment_sum(src, seg, n):
    return jax.ops.segment_sum(src, seg, n)
kernel_name = 'mk_flamingo_gated_d1_seqx_r2_c4f081'

def setup_inputs(seed: int=0):
    np.random.seed(seed)
    _w = jnp.asarray

    def _rec_inputs():
        import jax
        import jax.numpy as jnp
        _rk = jax.random.key(seed)
        x = 7.22e-05 + 1 * jax.random.normal(jax.random.fold_in(_rk, 1), (8, 100, 1024), jnp.float32)
        _lenS = 100 - jax.random.randint(jax.random.fold_in(_rk, 7), (8,), 0, max(1, 100 // 4) + 1, jnp.int32)
        _lenS2 = 722 - jax.random.randint(jax.random.fold_in(_rk, 8), (8,), 0, max(1, 722 // 4) + 1, jnp.int32)
        _ctx_512P = jax.random.normal(jax.random.fold_in(_rk, 11), (8, 16, 256), jnp.float32)
        _ctx_512c = jax.random.dirichlet(jax.random.fold_in(_rk, 511), 0.3 * jnp.ones((16,), jnp.float32), (8, 722))
        _ctx_512t = jnp.einsum('bsk,bkd->bsd', _ctx_512c, _ctx_512P)
        _ctx_512t = _ctx_512t * jax.lax.rsqrt(jnp.mean(jnp.square(_ctx_512t)) + 1e-12) * 0.953939
        ctx_512 = -0.000514642 + 1.00011 * (_ctx_512t + 0.3 * jax.random.normal(jax.random.fold_in(_rk, 611), (8, 722, 256), jnp.float32))
        _g = jax.random.normal(jax.random.fold_in(_rk, 9001), (2, 1), jnp.float32)
        _g = jnp.sign(_g) * jnp.maximum(jnp.abs(_g), 1.0) + (_g == 0) * 1.0
        g_xattn = _g[0]
        g_ffn = _g[1]
        return (x, ctx_512, g_xattn, g_ffn)
    x, ctx_512, g_xattn, g_ffn = _rec_inputs()

    def _L0_xattn_setup():
        import jax, jax.numpy as jnp
        import numpy as np
        B, S, H, NH, L = (2, 1024, 1024, 16, 256)
        HD = H // NH
        key = jax.random.key(seed)
        k1, k2, k3, k4, k5 = jax.random.split(key, 5)
        scale = 0.02
        return {'q': jax.random.normal(k1, (B, S, H), dtype=jnp.float32), 'latent_kv': jax.random.normal(k2, (B, S, L), dtype=jnp.float32), 'Wq': jax.random.normal(k3, (H, H), dtype=jnp.float32) * scale, 'Wkv_expand': jax.random.normal(k4, (2 * H, L), dtype=jnp.float32) * scale, 'Wout': jax.random.normal(k5, (H, H), dtype=jnp.float32) * scale}
    _L0_xattn_all = _L0_xattn_setup()
    _L0_xattn_in = {k: v for k, v in _L0_xattn_all.items() if k in ('Wq', 'Wkv_expand', 'Wout')}
    del _L0_xattn_all

    def _L0_ffn_setup():
        import jax, jax.numpy as jnp
        import numpy as np
        EPS = 1e-05

        def activation_quant(x):
            scale = 127.0 / jnp.clip(jnp.max(jnp.abs(x), axis=-1, keepdims=True), EPS, None)
            return jnp.clip(jnp.round(x * scale), -128.0, 127.0) / scale

        def weight_quant(w):
            scale = 1.0 / jnp.clip(jnp.mean(jnp.abs(w)), EPS, None)
            return jnp.clip(jnp.round(w * scale), -1.0, 1.0) / scale

        def bitlinear(x, w):
            xq = x + jax.lax.stop_gradient(activation_quant(x) - x)
            wq = w + jax.lax.stop_gradient(weight_quant(w) - w)
            return jnp.einsum('bsd,hd->bsh', xq, wq)
        key = jax.random.key(seed)
        k1, k2, k3 = jax.random.split(key, 3)
        B, S, D, H = (4, 1024, 1024, 4096)
        x = jax.random.normal(k1, (B, S, D), dtype=jnp.float32)
        w1 = jax.random.normal(k2, (H, D), dtype=jnp.float32) * 0.02
        w2 = jax.random.normal(k3, (D, H), dtype=jnp.float32) * 0.02
        return {'x': x, 'w1': w1, 'w2': w2}
    _L0_ffn_all = _L0_ffn_setup()
    _L0_ffn_in = {k: v for k, v in _L0_ffn_all.items() if k in ('w1', 'w2')}
    del _L0_ffn_all
    return {'x': x, 'ctx_512': ctx_512, 'g_xattn': g_xattn, 'g_ffn': g_ffn, 'L0_xattn_Wq': _L0_xattn_in['Wq'], 'L0_xattn_Wkv_expand': _L0_xattn_in['Wkv_expand'], 'L0_xattn_Wout': _L0_xattn_in['Wout'], 'L0_ffn_w1': _L0_ffn_in['w1'], 'L0_ffn_w2': _L0_ffn_in['w2']}

def reference(x, ctx_512, g_xattn, g_ffn, L0_xattn_Wq, L0_xattn_Wkv_expand, L0_xattn_Wout, L0_ffn_w1, L0_ffn_w2):
    import jax
    import jax.numpy as jnp

    def _L0_xattn_ref(q, latent_kv, Wq, Wkv_expand, Wout):
        import jax, jax.numpy as jnp
        import numpy as np
        B, S, H, NH, L = (2, 1024, 1024, 16, 256)
        HD = H // NH
        b, sq, _ = q.shape
        sk = latent_kv.shape[1]
        qp = q @ Wq.T
        kv = latent_kv @ Wkv_expand.T
        k, v = jnp.split(kv, 2, axis=-1)
        qh = qp.reshape(b, sq, NH, HD).transpose(0, 2, 1, 3)
        kh = k.reshape(b, sk, NH, HD).transpose(0, 2, 1, 3)
        vh = v.reshape(b, sk, NH, HD).transpose(0, 2, 1, 3)
        inv_sqrt_d = 1.0 / jnp.sqrt(jnp.float32(HD))
        scores = jnp.einsum('bhqd,bhkd->bhqk', qh, kh) * inv_sqrt_d
        causal = jnp.tril(jnp.ones((sq, sk), dtype=bool))
        scores = jnp.where(causal, scores, jnp.finfo(scores.dtype).min)
        attn = jax.nn.softmax(scores, axis=-1)
        out = jnp.einsum('bhqk,bhkd->bhqd', attn, vh)
        out = out.transpose(0, 2, 1, 3).reshape(b, sq, H)
        return out @ Wout.T

    def _L0_ffn_ref(x, w1, w2):
        import jax, jax.numpy as jnp
        import numpy as np
        EPS = 1e-05

        def activation_quant(x):
            scale = 127.0 / jnp.clip(jnp.max(jnp.abs(x), axis=-1, keepdims=True), EPS, None)
            return jnp.clip(jnp.round(x * scale), -128.0, 127.0) / scale

        def weight_quant(w):
            scale = 1.0 / jnp.clip(jnp.mean(jnp.abs(w)), EPS, None)
            return jnp.clip(jnp.round(w * scale), -1.0, 1.0) / scale

        def bitlinear(x, w):
            xq = x + jax.lax.stop_gradient(activation_quant(x) - x)
            wq = w + jax.lax.stop_gradient(weight_quant(w) - w)
            return jnp.einsum('bsd,hd->bsh', xq, wq)
        h = bitlinear(x, w1)
        h = jax.nn.gelu(h, approximate=False)
        return bitlinear(h, w2)
    x = x + jnp.tanh(g_xattn[0]) * _L0_xattn_ref(_layernorm(x, axis=-1), ctx_512, L0_xattn_Wq, L0_xattn_Wkv_expand, L0_xattn_Wout)
    x = x + jnp.tanh(g_ffn[0]) * _L0_ffn_ref(_layernorm(x, axis=-1), L0_ffn_w1, L0_ffn_w2)
    return x

_drawn_inputs = setup_inputs


def setup_inputs(seed=0):
    import zlib

    import numpy as np

    out = dict(_drawn_inputs(seed))
    spreads = {}
    factors = {'L0_xattn_Wq': 5.011}
    for name, (base, spread) in spreads.items():
        noise = np.random.default_rng([zlib.crc32(name.encode()), seed]).standard_normal(out[name].shape)
        drawn = base * np.exp(spread * noise) if base else spread * noise
        out[name] = jnp.asarray(drawn.astype(out[name].dtype))
    for name, factor in factors.items():
        out[name] = (out[name] * factor).astype(out[name].dtype)
    return out
```

```python
from contextlib import ExitStack

import concourse.bass as bass
from concourse import mybir

F32 = mybir.dt.float32
BF16 = mybir.dt.bfloat16
F8 = mybir.dt.float8e4
I16 = mybir.dt.int16
ALU = mybir.AluOpType
ACT = mybir.ActivationFunctionType
AX = mybir.AxisListType

P = 128
B, S, H = 8, 100, 1024
L = 256
HD = 64
F = 4096
N = B * S
HALF = N // 2
HB = B // 2
KC = H // P
LC = L // P
FC = F // P
LN_EPS = 1e-5
Q_EPS = 1e-5
Q_MAX = 127.0
NEG = -3.0e38

NSTAGE = 4
NTILE = FC
NWI = 3
HG = 4
HSLOTS = FC + HG
NGROUP = 4 * KC


def flamingo_layer(nc, x_tok, x_t, ctx_t, wqkv, wout, w1, w2, g_attn, g_ffn, out_t):
    with ExitStack() as ctx:
        def sb(name, shape, dt):
            return ctx.enter_context(nc.sbuf_tensor(name, shape, dt))

        def sem(name):
            return ctx.enter_context(nc.semaphore(name))

        region_x = sb("region_x", [P, KC * N], F32)
        xn_T = region_x[:].rearrange("p (c t) -> p c t", c=KC)
        x2_T = xn_T
        region_aw = sb("region_aw", [P, max(KC * N + KC * H, HSLOTS * HALF)], F32)
        attn_T = region_aw[:, 0:KC * N].rearrange("p (c t) -> p c t", c=KC)
        wout_sb = region_aw[:, KC * N:KC * N + KC * H].rearrange("p (o k m) -> p o k m", o=KC, k=KC)
        h_ring = region_aw[:, 0:HSLOTS * HALF].rearrange("p (s t) -> p s t", s=HSLOTS)
        region_w1 = sb("region_w1", [P, B * H], F32)
        x_rows = region_w1[0:S, :].rearrange("p (b f) -> p b f", b=B)
        w1_q = region_w1[:].bitcast(F8).rearrange("p (j k m) -> p j k m", j=FC, k=KC)
        hq_b = region_w1[:, 0:FC * HALF // 2].bitcast(BF16).rearrange("p (j t) -> p j t", j=FC)
        region_w2 = sb("region_w2", [P, B * H], F32)
        QKV_COLS = (KC + 2 * LC) * P
        wqkv_sb = region_w2[:, 0:2 * QKV_COLS].rearrange("p (r k m) -> p r k m", r=2, m=P)
        w2_q = region_w2[:].bitcast(F8).rearrange("p (o k m) -> p o k m", o=KC, k=FC)
        region_h = sb("region_h", [P, FC * HALF // 2], F32)
        q_T = region_h[:, 0:2 * N].rearrange("p (r t) -> p r t", r=2)
        k_T = region_h[:, 2 * N:4 * N].rearrange("p (r t) -> p r t", r=2)
        v_rows = region_h[0:S, 4 * N:4 * N + 2 * B * P].rearrange("p (r b f) -> p r b f", r=2, b=B)
        xc_rows = region_h[0:S, 0:HB * H].rearrange("p (b f) -> p b f", b=HB)
        xi_rows = region_h[0:S, HB * H:HB * H + H].bitcast(I16).rearrange("p (r f) -> p r f", r=2)
        xb_rows = region_h[0:S, HB * H + H:HB * H + 2 * H].bitcast(BF16).rearrange("p (r f) -> p r f", r=2)
        hq_a = region_h[:].bitcast(BF16).rearrange("p (j t) -> p j t", j=FC)
        hq = [hq_a, hq_b]
        NSM = 3
        region_q = sb("region_q", [P, KC * N // 2], F32)
        sm = region_q[0:S, 0:NSM * HALF].rearrange("p (r b k) -> p r b k", r=NSM, b=HB)
        pT = region_q[0:S, NSM * HALF:(NSM + 2) * HALF].rearrange("p (r t) -> p r t", r=2)
        xq_T = region_q[:].bitcast(BF16).rearrange("p (c t) -> p c t", c=KC)
        region_c = sb("region_c", [P, LC * N], F32)
        ctx_sb = region_c[:].rearrange("p (c t) -> p c t", c=LC)
        d_bc = region_c[:, 0:N].rearrange("p (r t) -> p r t", r=2)
        s_bc = region_c[:, N:N + HALF]
        run = region_c[:, N + HALF:N + 2 * HALF]
        stage = sb("stage", [P, NSTAGE, H], F32)
        e_bc = stage[:, 0, 0:2 * HALF].rearrange("p (r t) -> p r t", r=2)
        region_i = sb("region_i", [P, NWI * H], I16)
        wint = region_i[:].rearrange("p (r m) -> p r m", r=NWI)
        hint = region_i[:, 0:2 * HALF].rearrange("p (r t) -> p r t", r=2)
        y_sb = region_i[:, 2 * HALF:6 * HALF].bitcast(F32).rearrange("p (r t) -> p r t", r=2)
        run4 = sb("run4", [P, HALF], F32)
        diag = sb("diag", [S, 2, HALF], F32)
        ident = sb("ident", [P, P], F32)
        ident_b = sb("ident_b", [P, P], BF16)
        ones = sb("ones", [P, P], F32)
        mask = sb("mask", [S, S], F32)
        bn = sb("bn", [S, B, 2, 6], F32)
        mv = sb("mv", [S, B, 2], F32)
        tiny = sb("tiny", [S, 8, B], F32)
        smax = sb("smax", [S, 2, HB], F32)
        ssum = sb("ssum", [S, 2, HB], F32)
        srcp = sb("srcp", [S, 2, HB], F32)
        gates = sb("gates", [P, 2], F32)
        gt = sb("gt", [P, 2], F32)
        wsum = sb("wsum", [P, 2, NTILE], F32)
        wtot = sb("wtot", [P, 2, 4], F32)
        bank = [ctx.enter_context(nc.psum_tensor(f"bank{i}", [P, 512], F32)) for i in range(8)]

        x_in = [sem(f"x_in{b}") for b in range(B)]
        ctx_in, g_in, wout_in, xT_in = (sem(n) for n in ("ctx_in", "g_in", "wout_in", "xT_in"))
        y_out = [sem(f"y_out{r}") for r in range(2)]
        wqkv_in = [sem(f"wqkv_in{r}") for r in range(2)]
        stage_in = [sem(f"stage_in{r}") for r in range(NSTAGE)]
        (consts_made, dve_own, act_own, pool_own, ln1_var, ln1_sd, x_normed, tr1_done, xn_act, xn_dve,
         proj_done, qk_out, v_out, scores_done, masked, max_done, shifted, exp_done, rcp_done, normed,
         p_turned, pT_out, pv_done, attn_out, abs_done, sums_done, tot_done, scale_done, w_int, w_quant,
         o_done, x2_out, x2_turned, mean_done, xc_done, ln2_var, ln2_sd, k_done, xi_done, xb_done, xq_turned,
         xq_out, d_diag, d_done, d_out, f1_done, f1_scaled, h_done, run_done, run_turned, se_diag, se_done,
         s_out, h_mul, h_int, hq_done, f2_done, y_scaled, y_added, gate_done) = (sem(n) for n in (
            "consts_made", "dve_own", "act_own", "pool_own", "ln1_var", "ln1_sd", "x_normed", "tr1_done",
            "xn_act", "xn_dve", "proj_done", "qk_out", "v_out", "scores_done", "masked", "max_done", "shifted",
            "exp_done", "rcp_done", "normed", "p_turned", "pT_out", "pv_done", "attn_out", "abs_done",
            "sums_done", "tot_done", "scale_done", "w_int", "w_quant", "o_done", "x2_out", "x2_turned",
            "mean_done", "xc_done", "ln2_var", "ln2_sd", "k_done", "xi_done", "xb_done", "xq_turned", "xq_out",
            "d_diag", "d_done", "d_out", "f1_done", "f1_scaled", "h_done", "run_done", "run_turned", "se_diag",
            "se_done", "s_out", "h_mul", "h_int", "hq_done", "f2_done", "y_scaled", "y_added", "gate_done"))

        UNITS = 6
        SLOT_UNITS = [(0,), (1,), (2, 3), (4, 5)]

        def proj_bank_free(e, u):
            if u < 3:
                if u == 0:
                    e.wait_ge(xn_act, KC)
                    e.wait_ge(xn_dve, KC)
                return
            c, i = divmod(u - 3, UNITS)
            if c >= KC:
                e.wait_ge(x2_out, u - 3 - KC * UNITS + 1)
            elif i < 4:
                e.wait_ge(qk_out, 4 * c + i + 1)
            else:
                e.wait_ge(v_out, 2 * c + i - 3)

        NT = 4 * NTILE
        PER = 3

        def slot_of(n):
            p, i = divmod(n, NTILE)
            return (0, 12, 22, 34)[p] + i // (PER, PER, PER, 2)[p]

        tiles_of = {}
        for n in range(NT):
            tiles_of.setdefault(slot_of(n), []).append(n)
        SUM_SLOT = {11: 0, 33: 1}
        LAST_SLOT = slot_of(NT - 1)

        def stage_wait(e, n):
            e.wait_ge(stage_in[n % NSTAGE], 16 * (n // NSTAGE + 1))

        def stage_free(e, n):
            m = n - NSTAGE
            if m < 0:
                return
            p, i = divmod(m, NTILE)
            if p % 2 == 0:
                e.wait_ge(abs_done, p // 2 * NTILE + i + 1)
            else:
                e.wait_ge(w_int, p // 2 * NTILE + i + 1)

        AT_BLOCK_PE = {1: [("x2", 4)], 3: [("x2", 5)], 5: [("x2", 6)], 7: [("x2", 7)], 14: [("xq", 4)],
                       15: [("xq", 5)], 17: [("xq", 6)], 19: [("xq", 7)], 20: [("d", 1)]}
        AT_BLOCK_DVE = {2: [("stats", 4)], 4: [("stats", 5), ("absmax", 4)], 6: [("stats", 6), ("absmax", 5)],
                        8: [("stats", 7), ("absmax", 6)], 9: [("absmax", 7), ("var", 1)], 11: [("scales", 1)],
                        13: [("cast", 4)], 14: [("cast", 5)], 16: [("cast", 6)], 18: [("cast", 7)]}
        AT_BLOCK_ACT = {2: [("centre", 4)], 4: [("centre", 5)], 6: [("centre", 6)], 8: [("centre", 7)],
                        10: [("root", 1)], 12: [("round", 4)], 13: [("round", 5)], 14: [("xq", 4)],
                        15: [("round", 6)], 16: [("xq", 5)], 17: [("round", 7)], 18: [("xq", 6)], 19: [("xq", 7)],
                        20: [("d", 1)]}

        block = ctx.enter_context(nc.Block())

        @block.sync
        def _(sp):
            for b in range(HB):
                sp.dma_start(x_rows[:, b, :], x_tok[b]).then_inc(x_in[b], 16)
            sp.dma_start(ctx_sb[:], ctx_t).then_inc(ctx_in, 16)
            sp.dma_start(wqkv_sb[:, 0], wqkv[0]).then_inc(wqkv_in[0], 16)
            for b in range(HB, B):
                sp.dma_start(x_rows[:, b, :], x_tok[b]).then_inc(x_in[b], 16)
            sp.dma_start(wqkv_sb[:, 1], wqkv[1]).then_inc(wqkv_in[1], 16)
            sp.dma_start(gates[:, 0:1], g_attn).then_inc(g_in, 16)
            sp.dma_start(gates[:, 1:2], g_ffn).then_inc(g_in, 16)
            for s in range(LAST_SLOT + 1):
                if s % 4 == 0 and 2 <= s // 4 + 1 < KC:
                    c = s // 4 + 1
                    sp.wait_ge(proj_done, UNITS * (c - 1))
                    sp.dma_start(wqkv_sb[:, c % 2], wqkv[c]).then_inc(wqkv_in[c % 2], 16)
                if 12 <= s < 12 + KC:
                    o = s - 12
                    sp.dma_start(wout_sb[:, o], wout[o]).then_inc(wout_in, 16)
                for n in tiles_of.get(s, []):
                    p, i = divmod(n, NTILE)
                    stage_free(sp, n)
                    sp.dma_start(stage[:, n % NSTAGE, :], (w1, w2)[p // 2][i]).then_inc(stage_in[n % NSTAGE], 16)
            for half in range(2):
                for o in range(KC):
                    u = KC * half + o
                    sp.wait_ge(y_added, u + 1)
                    sp.dma_start(out_t[o, :, half * HALF:(half + 1) * HALF], y_sb[:, u % 2, :])\
                        .then_inc(y_out[u % 2], 16)
            for r in range(2):
                sp.wait_ge(y_out[r], 16 * KC)

        @block.gpsimd
        def _(pool):
            pool.memset(ident[:], 0.0).then_inc(pool_own, 1)
            pool.memset(ident_b[:], 0.0).then_inc(pool_own, 1)
            pool.memset(mask[:], 0.0).then_inc(pool_own, 1)
            pool.memset(ones[:], 1.0).then_inc(consts_made, 1)
            pool.wait_ge(pool_own, 3)
            for m in (ident, ident_b):
                pool.affine_select(out=m[:], in_=m[:], compare_op=ALU.not_equal, fill=1.0, base=0,
                                   pattern=[[-1, P]], channel_multiplier=1).then_inc(consts_made, 1)
            pool.affine_select(out=mask[:], in_=mask[:], compare_op=ALU.is_ge, fill=NEG, base=0,
                               pattern=[[-1, S]], channel_multiplier=1).then_inc(consts_made, 1)

            def round_tile(n):
                p, i = divmod(n, NTILE)
                t = p // 2 * NTILE + i
                stage_wait(pool, n)
                if i == 0:
                    pool.wait_ge(scale_done, p // 2 + 1)
                if t >= NWI:
                    pool.wait_ge(w_quant, t - NWI + 1)
                nc.gpsimd.tensor_scalar(wint[:, t % NWI, :], stage[:, n % NSTAGE, :], wtot[:, p // 2, 2:3], 0.0,
                                        ALU.mult, ALU.add).then_inc(w_int, 1)

            for s in range(LAST_SLOT + 1):
                if s < NGROUP:
                    r = s % NSM
                    pool.wait_ge(max_done, s + 1)
                    nc.gpsimd.tensor_tensor(sm[:, r], sm[:, r], smax[:, s % 2, :].to_broadcast([S, HB, S]),
                                            ALU.subtract).then_inc(shifted, 1)
                tiles = [n for n in tiles_of.get(s, []) if n // NTILE % 2 == 1]
                for n in tiles[0:1]:
                    round_tile(n)
                if s < NGROUP:
                    pool.wait_ge(rcp_done, s + 1)
                    nc.gpsimd.tensor_tensor(sm[:, r], sm[:, r], srcp[:, s % 2, :].to_broadcast([S, HB, S]),
                                            ALU.mult).then_inc(normed, 1)
                for n in tiles[1:]:
                    round_tile(n)
            for half in range(2):
                pool.wait_ge(s_out, half + 1)
                for j in range(FC):
                    q = half * FC + j
                    pool.wait_ge(h_done, q + 1)
                    h = h_ring[:, q % HSLOTS, :]
                    nc.gpsimd.tensor_tensor(h, h, s_bc, ALU.mult).then_inc(h_mul, 1)

        @block.scalar
        def _(act):
            def root(dst, src):
                return nc.scalar.activation(dst, src, ACT.Sqrt)

            for half in range(2):
                act.wait_ge(ln1_var, half + 1)
                root(tiny[:, 1, half * HB:(half + 1) * HB], tiny[:, 0, half * HB:(half + 1) * HB]).then_inc(ln1_sd, 1)
            for half in range(2):
                for c in range(0, KC, 2):
                    act.wait_ge(tr1_done, half * KC + c + 1)
                    nc.scalar.copy(xn_T[:, c, half * HALF:(half + 1) * HALF], bank[c][:, 0:HALF]).then_inc(xn_act, 1)
            act.wait_ge(g_in, 32)
            nc.scalar.activation(gt[:], gates[:], ACT.Tanh).then_inc(gate_done, 1)

            def copy_unit(c, i):
                u = UNITS * c + i
                half = i % 2
                act.wait_ge(proj_done, u + 1)
                dst = (q_T, k_T)[i // 2]
                if c >= 2:
                    act.wait_ge(scores_done, 4 * (c - 1))
                nc.scalar.mul(dst[:, c % 2, half * HALF:(half + 1) * HALF], bank[u % 3][:, 0:HALF],
                              (HD ** -0.5, 1.0)[i // 2]).then_inc(qk_out, 1)

            def abs_tile(n):
                p, i = divmod(n, NTILE)
                stage_wait(act, n)
                w = stage[:, n % NSTAGE, :]
                if p // 2 * NTILE + i > 0:
                    act.wait_ge(abs_done, p // 2 * NTILE + i)
                nc.scalar.activation(w, w, ACT.Abs, accum_out=wsum[:, p // 2, i:i + 1]).then_inc(abs_done, 1)

            for i in range(4):
                copy_unit(0, i)
            for s in range(LAST_SLOT + 1):
                c = s // 4 + 1
                if c < KC:
                    for i in SLOT_UNITS[s % 4]:
                        if i < 4:
                            copy_unit(c, i)
                if 1 <= s <= NGROUP:
                    g = s - 1
                    act.wait_ge(p_turned, g + 1)
                    if g >= 2:
                        act.wait_ge(pv_done, g - 1)
                    nc.scalar.copy(pT[:, g % 2, :], bank[5 + g % 2][0:S, 0:HALF]).then_inc(pT_out, 1)
                if 3 <= s <= NGROUP + 1 and s % 2 == 1:
                    q = (s - 3) // 2
                    act.wait_ge(pv_done, 2 * q + 2)
                    nc.scalar.copy(attn_T[:, q // 2, (q % 2) * HALF:(q % 2 + 1) * HALF], bank[7][:, 0:HALF])\
                        .then_inc(attn_out, 1)
                if s < NGROUP:
                    act.wait_ge(shifted, s + 1)
                    nc.scalar.activation(sm[:, s % NSM], sm[:, s % NSM], ACT.Exp).then_inc(exp_done, 1)
                if s == 26:
                    act.wait_ge(proj_done, UNITS * (KC - 1) + 2)
                    act.dma_start(x2_T, x_t).then_inc(xT_in, 16)
                for n in tiles_of.get(s, []):
                    if n // NTILE % 2 == 0:
                        abs_tile(n)

            def centre(n):
                act.wait_ge(mean_done, n + 1)
                if n == 0:
                    act.wait_ge(pv_done, NGROUP)
                if n == HB:
                    act.wait_ge(xi_done, HB)
                for t in range(2):
                    ins = nc.scalar.activation(xc_rows[:, n % HB, t * 512:(t + 1) * 512],
                                               bank[3 + 2 * (n % 2) + t][0:S, :], ACT.Identity,
                                               bias=tiny[:, 7, n:n + 1])
                ins.then_inc(xc_done, 1)

            def ln2_root(half):
                act.wait_ge(ln2_var, half + 1)
                hs = slice(half * HB, (half + 1) * HB)
                root(tiny[:, 1, hs], tiny[:, 0, hs]).then_inc(ln2_sd, 1)

            def round_x(n):
                act.wait_ge(k_done, n // HB + 1)
                if n >= 2:
                    act.wait_ge(xb_done, n - 1)
                nc.scalar.activation(xi_rows[:, n % 2, :], xc_rows[:, n % HB, :], ACT.Copy,
                                     scale=tiny[:, 5, n:n + 1]).then_inc(xi_done, 1)

            def copy_xq(n):
                act.wait_ge(xq_turned, n + 1)
                src = bank[7][:, 0:KC * S // 2].bitcast(BF16).rearrange("p (c t) -> p c t", c=KC)
                nc.scalar.copy(xq_T[:, :, n * S:(n + 1) * S], src).then_inc(xq_out, 1)

            def copy_d(half):
                act.wait_ge(d_done, half + 1)
                nc.scalar.copy(d_bc[:, half, :], bank[7][:, 0:HALF]).then_inc(d_out, 1)

            def gelu(half, j):
                q = half * FC + j
                act.wait_ge(f1_scaled, q + 1)
                if q >= HSLOTS:
                    act.wait_ge(h_int, q - HSLOTS + 1)
                elif q == 0:
                    act.wait_ge(o_done, 2 * KC)
                nc.scalar.activation(h_ring[:, q % HSLOTS, :], bank[q % 3][:, 0:HALF], ACT.Gelu).then_inc(h_done, 1)

            def round_h(q):
                act.wait_ge(h_mul, q + 1)
                if q == 0:
                    act.wait_ge(w_quant, 2 * NTILE)
                if q >= 2:
                    act.wait_ge(hq_done, q - 1)
                nc.scalar.copy(hint[:, q % 2, :], h_ring[:, q % HSLOTS, :]).then_inc(h_int, 1)

            def copy_s(half):
                act.wait_ge(se_done, half + 1)
                if half == 0:
                    act.wait_ge(w_int, 2 * NTILE)
                else:
                    act.wait_ge(h_mul, FC)
                nc.scalar.copy(s_bc, bank[3][:, 0:HALF])
                nc.scalar.copy(e_bc[:, half, :], bank[4][:, 0:HALF]).then_inc(s_out, 1)

            for n in range(HB):
                centre(n)
            ln2_root(0)
            round_x(0)
            for n in range(HB):
                if n + 1 < HB:
                    round_x(n + 1)
                copy_xq(n)
            copy_d(0)
            for j in range(FC):
                gelu(0, j)
                for step, n in AT_BLOCK_ACT.get(j, []):
                    (centre if step == "centre" else round_x if step == "round" else
                     copy_xq if step == "xq" else copy_d if step == "d" else ln2_root)(n)
            for j in range(FC):
                if j >= HG:
                    round_h(j - HG)
                gelu(1, j)
                if j == 3:
                    copy_s(0)
            for j in range(FC - HG, FC):
                round_h(j)
            copy_s(1)
            for j in range(FC):
                round_h(FC + j)

        @block.vector
        def _(dve):
            count = [0]

            def link(ins):
                count[0] += 1
                ins.then_inc(dve_own, 1)
                dve.wait_ge(dve_own, count[0])

            def masked_(ins):
                ins.then_inc(masked, 1)
                dve.wait_ge(masked, s + 1)

            def inv_root(hs):
                ve, sd, r, t = (tiny[:, i, hs] for i in range(4))
                link(nc.vector.reciprocal(r, sd))
                link(nc.vector.tensor_tensor(t, r, r, ALU.mult))
                link(nc.vector.tensor_tensor(t, t, ve, ALU.mult))
                link(nc.vector.tensor_scalar(t, t, -0.5, 1.5, ALU.mult, ALU.add))
                link(nc.vector.tensor_tensor(r, r, t, ALU.mult))

            for half in range(2):
                hs = slice(half * HB, (half + 1) * HB)
                for b in range(half * HB, (half + 1) * HB):
                    dve.wait_ge(x_in[b], 16)
                    for t in range(2):
                        last = nc.vector.bn_stats(bn[:, b, t, :], x_rows[:, b, t * 512:(t + 1) * 512])
                    link(last)
                    link(nc.vector.bn_aggr(mv[:, b, :], bn[:, b, :, :]))
                nc.vector.tensor_scalar(tiny[:, 0, hs], mv[:, hs, 1], LN_EPS, None, ALU.add).then_inc(ln1_var, 1)
                dve.wait_ge(ln1_sd, half + 1)
                inv_root(hs)
                for b in range(half * HB, (half + 1) * HB):
                    nc.vector.tensor_scalar(x_rows[:, b, :], x_rows[:, b, :], mv[:, b, 0:1], tiny[:, 2, b:b + 1],
                                            ALU.subtract, ALU.mult).then_inc(x_normed, 1)
            for half in range(2):
                for c in range(1, KC, 2):
                    dve.wait_ge(tr1_done, half * KC + c + 1)
                    nc.vector.tensor_copy(xn_T[:, c, half * HALF:(half + 1) * HALF], bank[c][:, 0:HALF])\
                        .then_inc(xn_dve, 1)

            def copy_v(c, half):
                u = UNITS * c + 4 + half
                dve.wait_ge(proj_done, u + 1)
                if c >= 2:
                    dve.wait_ge(pv_done, 4 * (c - 1))
                nc.vector.tensor_copy(v_rows[:, c % 2, half * HB:(half + 1) * HB, :],
                                      bank[u % 3][0:S, :].rearrange("p (b f) -> p b f", b=HB)).then_inc(v_out, 1)

            def clip_tile(n):
                p, i = divmod(n, NTILE)
                t = p // 2 * NTILE + i
                dve.wait_ge(w_int, t + 1)
                if t == 0:
                    dve.wait_ge(tr1_done, 2 * KC)
                if t == NTILE:
                    dve.wait_ge(proj_done, UNITS * KC)
                wq = (w1_q, w2_q)[p // 2]
                dst = wq[:, i] if p < 2 else wq[:, i // 4, i % 4 * KC:(i % 4 + 1) * KC]
                nc.vector.tensor_scalar(dst, wint[:, t % NWI, :].rearrange("p (k m) -> p k m", k=KC), 1.0, -1.0,
                                        ALU.min, ALU.max, saturate=False).then_inc(w_quant, 1)

            def sum_columns(w):
                dve.wait_ge(abs_done, NTILE * (w + 1))
                nc.vector.tensor_reduce(wtot[:, w, 0:1], wsum[:, w, :], AX.X, ALU.add).then_inc(sums_done, 1)

            def finish_scale(w):
                dve.wait_ge(tot_done, w + 1)
                link(nc.vector.tensor_scalar(wtot[:, w, 1:2], bank[7][:, 0:1], 1.0 / (F * H), Q_EPS,
                                             ALU.mult, ALU.max))
                link(nc.vector.reciprocal(wtot[:, w, 2:3], wtot[:, w, 1:2]))
                nc.vector.tensor_scalar(wtot[:, w, 3:4], wtot[:, w, 1:2], 1.0 / Q_MAX, None, ALU.mult)\
                    .then_inc(scale_done, 1)

            for half in range(2):
                copy_v(0, half)
            for s in range(NGROUP):
                c = s // 4 + 1
                if SUM_SLOT.get(s - 1) is not None:
                    finish_scale(SUM_SLOT[s - 1])
                if s % 4 == 3 and c < KC:
                    for half in range(2):
                        copy_v(c, half)
                r = s % NSM
                dve.wait_ge(scores_done, s + 1)
                if s == 0:
                    dve.wait_ge(consts_made, 4)
                if s >= NSM:
                    dve.wait_ge(p_turned, s - NSM + 1)
                masked_(nc.vector.tensor_tensor(sm[:, r], bank[3 + s % 2][0:S, 0:HALF].rearrange("p (b k) -> p b k", b=HB),
                                             mask[:].unsqueeze(1).to_broadcast([S, HB, S]), ALU.add))
                if s >= 2:
                    dve.wait_ge(shifted, s - 1)
                nc.vector.tensor_reduce(smax[:, s % 2, :], sm[:, r], AX.X, ALU.max).then_inc(max_done, 1)
                for n in tiles_of.get(s - 1, []):
                    if n // NTILE % 2 == 1:
                        clip_tile(n)
                if s in SUM_SLOT:
                    sum_columns(SUM_SLOT[s])
                dve.wait_ge(exp_done, s + 1)
                link(nc.vector.tensor_reduce(ssum[:, s % 2, :], sm[:, r], AX.X, ALU.add))
                if s >= 2:
                    dve.wait_ge(normed, s - 1)
                nc.vector.reciprocal(srcp[:, s % 2, :], ssum[:, s % 2, :]).then_inc(rcp_done, 1)

            def gated_add(u):
                half, o = divmod(u, KC)
                dve.wait_ge(o_done, u + 1)
                if u == 0:
                    dve.wait_ge(xT_in, 16)
                    dve.wait_ge(gate_done, 1)
                x2 = x2_T[:, o, half * HALF:(half + 1) * HALF]
                nc.vector.scalar_tensor_tensor(x2, bank[u % 3][:, 0:HALF], gt[:, 0:1], x2, ALU.mult, ALU.add)\
                    .then_inc(x2_out, 1)

            def ln2_stats(n):
                dve.wait_ge(x2_turned, n + 1)
                for t in range(2):
                    last = nc.vector.bn_stats(bn[:, n, t, :], bank[3 + 2 * (n % 2) + t][0:S, :])
                link(last)
                link(nc.vector.bn_aggr(mv[:, n, :], bn[:, n, :, :]))
                nc.vector.tensor_scalar(tiny[:, 7, n:n + 1], mv[:, n, 0:1], -1.0, None, ALU.mult).then_inc(mean_done, 1)

            def ln2_absmax(n):
                dve.wait_ge(xc_done, n + 1)
                link(nc.vector.tensor_reduce(tiny[:, 4, n:n + 1], xc_rows[:, n % HB, :], AX.X, ALU.max,
                                             apply_absolute_value=True))

            def ln2_var_step(half):
                hs = slice(half * HB, (half + 1) * HB)
                nc.vector.tensor_scalar(tiny[:, 0, hs], mv[:, hs, 1], LN_EPS, None, ALU.add).then_inc(ln2_var, 1)

            def ln2_scales(half):
                hs = slice(half * HB, (half + 1) * HB)
                dve.wait_ge(ln2_sd, half + 1)
                inv_root(hs)
                r, t, am, k, d = (tiny[:, i, hs] for i in (2, 3, 4, 5, 6))
                link(nc.vector.tensor_tensor(am, am, r, ALU.mult))
                link(nc.vector.tensor_scalar(am, am, Q_EPS, None, ALU.max))
                link(nc.vector.reciprocal(t, am))
                nc.vector.scalar_tensor_tensor(k, t, Q_MAX, r, ALU.mult, ALU.mult).then_inc(k_done, 1)
                link(nc.vector.tensor_scalar(d, am, wtot[0:S, 0, 3:4], None, ALU.mult))
                if half:
                    dve.wait_ge(d_done, 1)
                spread(0, d).then_inc(d_diag, 1)

            def spread(r, v):
                return nc.vector.tensor_tensor(diag[:, r, :].rearrange("p (b k) -> p b k", b=HB),
                                               ident[0:S, 0:S].unsqueeze(1).to_broadcast([S, HB, S]),
                                               v.to_broadcast([S, HB, S]), ALU.mult)

            def cast_x(n):
                dve.wait_ge(xi_done, n + 1)
                if n >= 2:
                    dve.wait_ge(xq_turned, n - 1)
                nc.vector.tensor_copy(xb_rows[:, n % 2, :], xi_rows[:, n % 2, :]).then_inc(xb_done, 1)

            for u in range(2 * KC):
                gated_add(u)
                if u == 0:
                    sum_columns(1)
                if u == 1:
                    finish_scale(1)
                if u >= 2:
                    for n in tiles_of[34 + u - 2]:
                        clip_tile(n)
                o = u - KC
                if 1 <= o <= 4:
                    ln2_stats(o - 1)
                if 2 <= o <= 5:
                    ln2_absmax(o - 2)
                if o == 4:
                    ln2_var_step(0)
                if o == 5:
                    ln2_scales(0)
                    cast_x(0)
                    cast_x(1)
                if o == 6:
                    cast_x(2)
                if o == 7:
                    cast_x(3)
            for s in (48, 49):
                for n in tiles_of[s]:
                    clip_tile(n)

            def scale_block(q):
                dve.wait_ge(f1_done, q + 1)
                if q % FC == 0:
                    dve.wait_ge(d_out, q // FC + 1)
                nc.vector.tensor_tensor(bank[q % 3][:, 0:HALF], bank[q % 3][:, 0:HALF], d_bc[:, q // FC, :], ALU.mult)\
                    .then_inc(f1_scaled, 1)

            def run_max(g):
                dve.wait_ge(h_done, HG * (g + 1))
                r = HG * g % HSLOTS
                h = h_ring[:, r:r + HG, :].rearrange("p j t -> p t j")
                if g % (FC // HG) == 0:
                    if g:
                        dve.wait_ge(run_turned, 1)
                    nc.vector.tensor_reduce(run, h, AX.X, ALU.max, apply_absolute_value=True).then_inc(run_done, 1)
                else:
                    link(nc.vector.tensor_reduce(run4[:], h, AX.X, ALU.max, apply_absolute_value=True))
                    dve.wait_ge(run_done, g)
                    nc.vector.tensor_tensor(run, run, run4[:], ALU.max).then_inc(run_done, 1)

            def cast_h(q):
                dve.wait_ge(h_int, q + 1)
                half, j = divmod(q, FC)
                if q == 0:
                    dve.wait_ge(xq_turned, B)
                if q == FC:
                    dve.wait_ge(f1_done, 2 * FC)
                nc.vector.tensor_copy(hq[half][:, j, :], hint[:, q % 2, :]).then_inc(hq_done, 1)

            def h_scales(half):
                dve.wait_ge(run_turned, half + 1)
                am, s, e = (tiny[:, i, 0:HB] for i in (4, 5, 6))
                link(nc.vector.tensor_reduce(am, bank[3][0:S, :].rearrange("p (b f) -> p b f", b=HB), AX.X, ALU.max))
                link(nc.vector.tensor_scalar(am, am, Q_EPS, None, ALU.max))
                link(nc.vector.reciprocal(s, am))
                link(nc.vector.tensor_scalar(s, s, Q_MAX, None, ALU.mult))
                link(nc.vector.tensor_scalar(e, am, wtot[0:S, 1, 3:4], gt[0:S, 1:2], ALU.mult, ALU.mult))
                dve.wait_ge(d_done, 2)
                if half:
                    dve.wait_ge(se_done, 1)
                spread(0, s).then_inc(se_diag, 1)
                spread(1, e).then_inc(se_diag, 1)

            for q in range(2 * FC):
                scale_block(q)
                if q >= FC + HG + 1:
                    cast_h(q - FC - HG - 1)
                if q % HG == 0 and q:
                    run_max(q // HG - 1)
                for step, n in AT_BLOCK_DVE.get(q, []):
                    (ln2_stats if step == "stats" else ln2_absmax if step == "absmax" else
                     ln2_var_step if step == "var" else ln2_scales if step == "scales" else cast_x)(n)
                if q == FC + 2:
                    h_scales(0)
            cast_h(FC - HG - 1)
            run_max(2 * FC // HG - 1)
            for j in range(FC - 4, FC):
                cast_h(j)
            h_scales(1)
            for u in range(2 * KC):
                if u < KC:
                    for j in range(4 * u - 4, 4 * u) if u < KC - 1 else range(4 * u - 4, FC):
                        if j >= 0:
                            cast_h(FC + j)
                half, o = divmod(u, KC)
                dve.wait_ge(f2_done, u + 1)
                dve.wait_ge(s_out, half + 1)
                if u >= 2:
                    dve.wait_ge(y_out[u % 2], 16 * (u // 2))
                y = y_sb[:, u % 2, :]
                nc.vector.tensor_tensor(y, bank[(2 * FC + u) % 3][:, 0:HALF], e_bc[:, half, :], ALU.mult)\
                    .then_inc(y_scaled, 1)
                dve.wait_ge(y_scaled, u + 1)
                nc.vector.tensor_tensor(y, y, x2_T[:, o, half * HALF:(half + 1) * HALF], ALU.add).then_inc(y_added, 1)

        @block.tensor
        def _(pe):
            pe.wait_ge(consts_made, 4)
            for half in range(2):
                pe.wait_ge(x_normed, HB * (half + 1))
                for c in range(KC):
                    if half:
                        pe.wait_ge((xn_act, xn_dve)[c % 2], c // 2 + 1)
                    for b in range(HB):
                        last = nc.tensor.transpose(bank[c][:, b * S:(b + 1) * S],
                                                   x_rows[:, half * HB + b, c * P:(c + 1) * P], ident[0:S, 0:S])
                    last.then_inc(tr1_done, 1)

            def half_of(v, half):
                return v[..., half * HALF:(half + 1) * HALF]

            def project(c, i):
                u = UNITS * c + i
                half = i % 2
                proj_bank_free(pe, u)
                if i == 0:
                    pe.wait_ge(wqkv_in[c % 2], 16 * (c // 2 + 1))
                if u == 2:
                    pe.wait_ge(ctx_in, 16)
                w = wqkv_sb[:, c % 2]
                if i < 2:
                    for k in range(KC):
                        last = nc.tensor.matmul(bank[u % 3][:, 0:HALF], w[:, k, :],
                                                xn_T[:, k, half * HALF:(half + 1) * HALF],
                                                start=(k == 0), stop=(k == KC - 1))
                elif i < 4:
                    for k in range(LC):
                        last = nc.tensor.matmul(bank[u % 3][:, 0:HALF], w[:, KC + k, :],
                                                ctx_sb[:, k, half * HALF:(half + 1) * HALF],
                                                start=(k == 0), stop=(k == LC - 1))
                else:
                    for b in range(HB):
                        n = half * HB + b
                        for k in range(LC):
                            last = nc.tensor.matmul(bank[u % 3][0:S, b * P:(b + 1) * P],
                                                    ctx_sb[:, k, n * S:(n + 1) * S], w[:, KC + LC + k, :],
                                                    start=(k == 0), stop=(k == LC - 1))
                last.then_inc(proj_done, 1)

            def scores(g):
                c, half, h = g // 4, g // 2 % 2, g % 2
                pe.wait_ge(qk_out, 4 * c + 3 + half)
                if g >= 2:
                    pe.wait_ge(masked, g - 1)
                rows = slice(HD * h, HD * (h + 1))
                for b in range(HB):
                    t = slice((half * HB + b) * S, (half * HB + b + 1) * S)
                    last = nc.tensor.matmul(bank[3 + g % 2][0:S, b * S:(b + 1) * S], q_T[rows, c % 2, t],
                                            k_T[rows, c % 2, t], start=True, stop=True)
                last.then_inc(scores_done, 1)

            def turn_p(g):
                pe.wait_ge(normed, g + 1)
                if g >= 2:
                    pe.wait_ge(pT_out, g - 1)
                for b in range(HB):
                    last = nc.tensor.transpose(bank[5 + g % 2][0:S, b * S:(b + 1) * S], sm[:, g % NSM, b, :],
                                               ident[0:S, 0:S])
                last.then_inc(p_turned, 1)

            def weigh_v(g):
                c, half, h = g // 4, g // 2 % 2, g % 2
                pe.wait_ge(pT_out, g + 1)
                pe.wait_ge(v_out, 2 * c + half + 1)
                if h == 0 and g:
                    pe.wait_ge(attn_out, g // 2)
                if g - 10 in (0,):
                    pe.wait_ge(scale_done, 1)
                for b in range(HB):
                    last = nc.tensor.matmul(bank[7][HD * h:HD * (h + 1), b * S:(b + 1) * S],
                                            v_rows[:, c % 2, half * HB + b, HD * h:HD * (h + 1)],
                                            pT[:, g % 2, b * S:(b + 1) * S], start=True, stop=True)
                last.then_inc(pv_done, 1)

            def total(w, groups):
                pe.wait_ge(attn_out, groups)
                pe.wait_ge(sums_done, w + 1)
                nc.tensor.matmul(bank[7][:, 0:1], ones[:], wtot[:, w, 0:1], start=True, stop=True).then_inc(tot_done, 1)

            def out_proj(u):
                half, o = divmod(u, KC)
                pe.wait_ge(attn_out, 2 * KC - 1 + half)
                if u == 0:
                    pe.wait_ge(wout_in, 16 * KC)
                if u < 3:
                    pe.wait_ge(v_out, 2 * KC)
                    pe.wait_ge(qk_out, 4 * KC)
                else:
                    pe.wait_ge(x2_out, u - 2)
                for k in range(KC):
                    last = nc.tensor.matmul(bank[u % 3][:, 0:HALF], wout_sb[:, o, k, :],
                                            attn_T[:, k, half * HALF:(half + 1) * HALF],
                                            start=(k == 0), stop=(k == KC - 1))
                last.then_inc(o_done, 1)

            def turn_x2(n):
                pe.wait_ge(x2_out, KC * (n // HB + 1))
                if n < 2:
                    pe.wait_ge((masked, pT_out)[n], NGROUP)
                else:
                    pe.wait_ge(xc_done, n - 1)
                for c in range(KC):
                    last = nc.tensor.transpose(bank[3 + 2 * (n % 2) + c // 4][0:S, c % 4 * P:(c % 4 + 1) * P],
                                               x2_T[:, c, n * S:(n + 1) * S], ident[:])
                last.then_inc(x2_turned, 1)

            def turn_xq(n):
                pe.wait_ge(xb_done, n + 1)
                if n == 0:
                    pe.wait_ge(scale_done, 2)
                elif n == HB:
                    pe.wait_ge(d_out, 1)
                else:
                    pe.wait_ge(xq_out, n)
                out = bank[7][:, 0:KC * S // 2].bitcast(BF16)
                for c in range(KC):
                    last = nc.tensor.transpose(out[:, c * S:(c + 1) * S], xb_rows[:, n % 2, c * P:(c + 1) * P],
                                               ident_b[0:S, 0:S])
                last.then_inc(xq_turned, 1)

            def spread_d(half):
                pe.wait_ge(d_diag, half + 1)
                pe.wait_ge(xq_out, HB * (half + 1))
                nc.tensor.matmul(bank[7][:, 0:HALF], ones[0:S, :], diag[:, 0, :], start=True, stop=True)\
                    .then_inc(d_done, 1)

            def hidden(q):
                half, j = divmod(q, FC)
                if q < 3:
                    pe.wait_ge(x2_out, 2 * KC)
                else:
                    pe.wait_ge(h_done, q - 2)
                if q == 0:
                    pe.wait_ge(w_quant, NTILE)
                if j == 0:
                    pe.wait_ge(xq_out, HB * (half + 1))
                for k in range(KC):
                    last = nc.tensor.matmul(bank[q % 3][:, 0:HALF], w1_q[:, j, k, :],
                                            xq_T[:, k, half * HALF:(half + 1) * HALF],
                                            start=(k == 0), stop=(k == KC - 1))
                last.then_inc(f1_done, 1)

            def turn_run(half):
                pe.wait_ge(run_done, FC // HG * (half + 1))
                for b in range(HB):
                    last = nc.tensor.transpose(bank[3][0:S, b * P:(b + 1) * P], run[:, b * S:(b + 1) * S], ident[:])
                last.then_inc(run_turned, 1)

            def spread_se(half):
                pe.wait_ge(se_diag, 2 * half + 2)
                nc.tensor.matmul(bank[3][:, 0:HALF], ones[0:S, :], diag[:, 0, :], start=True, stop=True)
                nc.tensor.matmul(bank[4][:, 0:HALF], ones[0:S, :], diag[:, 1, :], start=True, stop=True)\
                    .then_inc(se_done, 1)

            def output(u):
                half, o = divmod(u, KC)
                q = 2 * FC + u
                if u < 3:
                    pe.wait_ge(h_done, q - 2)
                else:
                    pe.wait_ge(y_scaled, u - 2)
                if u == 0:
                    pe.wait_ge(w_quant, 2 * NTILE)
                if o == 0:
                    pe.wait_ge(hq_done, FC * (half + 1))
                for k in range(FC):
                    last = nc.tensor.matmul(bank[q % 3][:, 0:HALF], w2_q[:, o, k, :], hq[half][:, k, :],
                                            start=(k == 0), stop=(k == FC - 1))
                    if u == 1 and k == KC:
                        spread_se(1)
                last.then_inc(f2_done, 1)

            for i in range(UNITS):
                project(0, i)
            for s in range(NGROUP + 2):
                c = s // 4 + 1
                if c < KC:
                    for i in SLOT_UNITS[s % 4]:
                        project(c, i)
                if s < NGROUP:
                    scores(s)
                else:
                    out_proj(s - NGROUP)
                if 1 <= s <= NGROUP:
                    turn_p(s - 1)
                if s >= 2:
                    weigh_v(s - 2)
                if s in SUM_SLOT:
                    total(SUM_SLOT[s], (s - 1) // 2)
            for u in range(2, 2 * KC):
                out_proj(u)
                o = u - KC
                if 0 <= o < HB:
                    turn_x2(o)
                if o in (6, 7):
                    turn_xq(2 * o - 12)
                    turn_xq(2 * o - 11)
            spread_d(0)
            for q in range(2 * FC):
                hidden(q)
                for step, n in AT_BLOCK_PE.get(q, []):
                    (turn_x2 if step == "x2" else turn_xq if step == "xq" else spread_d)(n)
                if q == FC + 1:
                    turn_run(0)
                if q == FC + 3:
                    spread_se(0)
            for u in range(2 * KC):
                output(u)
                if u == 0:
                    turn_run(1)


def kernel(x, ctx_512, g_xattn, g_ffn, L0_xattn_Wq, L0_xattn_Wkv_expand, L0_xattn_Wout, L0_ffn_w1, L0_ffn_w2):
    import numpy as np
    import concourse.bacc as bacc
    from concourse.bass_utils import run_bass_kernel_spmd

    def a(v):
        return np.asarray(v)

    x, ctxs = a(x), a(ctx_512)

    def tiles(w):
        o, i = w.shape
        return w.reshape(o // P, P, i // P, P).transpose(0, 3, 2, 1)

    wkv = a(L0_xattn_Wkv_expand)
    arrays = {
        "x_tok": x,
        "x_t": x.reshape(N, KC, P).transpose(2, 1, 0),
        "ctx_t": ctxs[:, :S].reshape(N, LC, P).transpose(2, 1, 0),
        "wqkv": np.concatenate([tiles(a(L0_xattn_Wq)), tiles(wkv[:H]), tiles(wkv[H:])], axis=2),
        "wout": tiles(a(L0_xattn_Wout)),
        "w1": tiles(a(L0_ffn_w1)),
        "w2": tiles(a(L0_ffn_w2)).reshape(KC, P, 4, KC * P).transpose(0, 2, 1, 3),
        "g_attn": np.broadcast_to(a(g_xattn).reshape(1, 1), (P, 1)),
        "g_ffn": np.broadcast_to(a(g_ffn).reshape(1, 1), (P, 1)),
    }
    arrays["w1"] = arrays["w1"].reshape(FC, P, H)
    arrays["w2"] = arrays["w2"].reshape(FC, P, H)
    arrays = {k: np.ascontiguousarray(v) for k, v in arrays.items()}
    nc = bacc.Bacc("TRN2", target_bir_lowering=False, num_devices=1, dynamic_dma_scratch_size=1024)
    aps = [nc.dram_tensor(k, v.shape, mybir.dt.from_np(v.dtype), kind="ExternalInput").ap() for k, v in arrays.items()]
    out = nc.dram_tensor("out_t", (KC, P, N), F32, kind="ExternalOutput").ap()
    flamingo_layer(nc, *aps, out)
    r = run_bass_kernel_spmd(nc, [arrays], core_ids=[0])
    got = r.results[0]["out_t"]
    return np.ascontiguousarray(got.reshape(H, N).T).reshape(B, S, H)
```

```python
from contextlib import ExitStack

import concourse.bass as bass
from concourse import mybir

F32 = mybir.dt.float32
BF16 = mybir.dt.bfloat16
F8 = mybir.dt.float8e4
F16 = mybir.dt.float16
I16 = mybir.dt.int16
I32 = mybir.dt.int32
ALU = mybir.AluOpType
ACT = mybir.ActivationFunctionType
AX = mybir.AxisListType

P = 128
B, S, H = 8, 100, 1024
L = 256
HD = 64
F = 4096
N = B * S
HALF = N // 2
HB = B // 2
KC = H // P
LC = L // P
FC = F // P
LN_EPS = 1e-5
Q_EPS = 1e-5
Q_MAX = 127.0
NEG = -3.0e38
TINY = 1e-30
EXPONENT = 0x7F800000
TOP = 2.0 ** 14
XN_SCALE = 2.0 ** 10

NSTAGE = 4
NTILE = FC
NWI = 3
NJOB = 2 * KC
HG = 4
HSLOTS = FC + HG
NGROUP = 4 * KC


def flamingo_layer(nc, x_tok, x_t, ctx_t, wq, wkv, wv, wout, w1, w2, g_attn, g_ffn, out_t):
    with ExitStack() as ctx:
        def sb(name, shape, dt):
            return ctx.enter_context(nc.sbuf_tensor(name, shape, dt))

        def sem(name):
            return ctx.enter_context(nc.semaphore(name))

        region_x = sb("region_x", [P, KC * N], F32)
        xn_T = region_x[:].bitcast(F16).rearrange("p (s c t) -> p s c t", s=2, c=KC)
        x2_T = region_x[:].rearrange("p (c t) -> p c t", c=KC)
        region_aw = sb("region_aw", [P, max(KC * N + KC * H, HSLOTS * HALF)], F32)
        attn_T = region_aw[:, 0:KC * N].bitcast(F16).rearrange("p (s c t) -> p s c t", s=2, c=KC)
        wout_p = region_aw[:, KC * N:KC * N + KC * H].bitcast(F16).rearrange("p (s o f) -> p s o f", s=2, o=KC)
        wv_all = region_aw[:, 0:LC * H]
        h_ring = region_aw[:, 0:HSLOTS * HALF].rearrange("p (s t) -> p s t", s=HSLOTS)
        region_w1 = sb("region_w1", [P, B * H], F32)
        x_rows = region_w1[0:S, :].rearrange("p (b f) -> p b f", b=B)
        w1_q = region_w1[:].bitcast(F8).rearrange("p (j k m) -> p j k m", j=FC, k=KC)
        hq_b = region_w1[:, 0:FC * HALF // 2].bitcast(BF16).rearrange("p (j t) -> p j t", j=FC)
        region_w2 = sb("region_w2", [P, B * H], F32)
        wq_raw = region_w2[:, 0:2 * H].rearrange("p (r f) -> p r f", r=2)
        wkv_sb = region_w2[:, 2 * H:3 * H].rearrange("p (r k m) -> p r k m", r=2, m=P)
        wq_p = region_w2[:, 3 * H:5 * H].bitcast(F16).rearrange("p (r s f) -> p r s f", r=2, s=2)
        wout_raw = region_w2[:, 5 * H:8 * H].rearrange("p (r f) -> p r f", r=3)
        w2_q = region_w2[:].bitcast(F8).rearrange("p (o k m) -> p o k m", o=KC, k=FC)
        region_h = sb("region_h", [P, FC * HALF // 2], F32)
        q_T = region_h[:, 0:2 * N].rearrange("p (r t) -> p r t", r=2)
        k_T = region_h[:, 2 * N:4 * N].rearrange("p (r t) -> p r t", r=2)
        v_rows = region_h[0:S, 4 * N:4 * N + 2 * B * P].rearrange("p (r b f) -> p r b f", r=2, b=B)
        xc_rows = region_h[0:S, 0:HB * H].rearrange("p (b f) -> p b f", b=HB)
        xi_rows = region_h[0:S, HB * H:HB * H + H].bitcast(I16).rearrange("p (r f) -> p r f", r=2)
        xb_rows = region_h[0:S, HB * H + H:HB * H + 2 * H].bitcast(BF16).rearrange("p (r f) -> p r f", r=2)
        hq_a = region_h[:].bitcast(BF16).rearrange("p (j t) -> p j t", j=FC)
        hq = [hq_a, hq_b]
        NSM = 4
        region_q = sb("region_q", [P, KC * N // 2], F32)
        sm = region_q[0:S, 0:NSM * HALF].rearrange("p (r b k) -> p r b k", r=NSM, b=HB)
        pT = region_q[0:S, NSM * HALF:(NSM + 2) * HALF].rearrange("p (r t) -> p r t", r=2)
        xq_T = region_q[:].bitcast(BF16).rearrange("p (c t) -> p c t", c=KC)
        region_c = sb("region_c", [P, LC * N], F32)
        ctx_sb = region_c[:].rearrange("p (c t) -> p c t", c=LC)
        d_bc = region_c[:, 0:N].rearrange("p (r t) -> p r t", r=2)
        s_bc = region_c[:, N:N + HALF]
        run = region_c[:, N + HALF:N + 2 * HALF]
        stage = sb("stage", [P, NSTAGE, H], F32)
        e_bc = stage[:, 0, 0:2 * HALF].rearrange("p (r t) -> p r t", r=2)
        region_i = sb("region_i", [P, NWI * H], I16)
        wint = region_i[:].rearrange("p (r m) -> p r m", r=NWI)
        hint = region_i[:, 0:2 * HALF].rearrange("p (r t) -> p r t", r=2)
        y_sb = region_i[:, 2 * HALF:6 * HALF].bitcast(F32).rearrange("p (r t) -> p r t", r=2)
        run4 = sb("run4", [P, HALF], F32)
        diag = sb("diag", [S, 2, HALF], F32)
        ident = sb("ident", [P, P], F32)
        ident_b = sb("ident_b", [P, P], BF16)
        ones = sb("ones", [P, P], F32)
        mask = sb("mask", [S, S], F32)
        bn = sb("bn", [S, B, 2, 6], F32)
        mv = sb("mv", [S, B, 2], F32)
        sums = sb("sums", [S, 2, B], F32)
        scratch = region_aw[0:S, LC * H:LC * H + H]
        tiny = sb("tiny", [S, 8, B], F32)
        smax = sb("smax", [S, 2, HB], F32)
        ssum = sb("ssum", [S, 2, HB], F32)
        srcp = sb("srcp", [S, 2, HB], F32)
        gates = sb("gates", [P, 2], F32)
        gt = sb("gt", [P, 2], F32)
        wsum = sb("wsum", [P, 2, NTILE], F32)
        wtot = sb("wtot", [P, 2, 4], F32)
        wm = sb("wm", [P, NJOB + 2], F32)
        wg = sb("wg", [P, NJOB + 2], F32)
        ws = sb("ws", [P, NJOB + 1], F32)
        wi = sb("wi", [P, NJOB + 1], F32)
        bank = [ctx.enter_context(nc.psum_tensor(f"bank{i}", [P, 512], F32)) for i in range(8)]

        x_in = [sem(f"x_in{b}") for b in range(B)]
        ctx_in, g_in, xT_in = (sem(n) for n in ("ctx_in", "g_in", "xT_in"))
        y_out = [sem(f"y_out{r}") for r in range(2)]
        wq_in = [sem(f"wq_in{r}") for r in range(2)]
        wkv_in = [sem(f"wkv_in{r}") for r in range(2)]
        wout_in = [sem(f"wout_in{r}") for r in range(3)]
        wm_done, wg_done, ws_done, w_hi, w_lo, attn_lo, xn_hi, xn_lo, ln1_act, ln1_ready, x_normed_pool, w_sign, wv_in, v_wm, v_wg, v_ws, act_own = (
            sem(n) for n in ("wm_done", "wg_done", "ws_done", "w_hi", "w_lo", "attn_lo", "xn_hi", "xn_lo",
                             "ln1_act", "ln1_ready", "x_normed_pool", "w_sign", "wv_in", "v_wm", "v_wg", "v_ws", "act_own"))
        stage_in = [sem(f"stage_in{r}") for r in range(NSTAGE)]
        (consts_made, dve_own, pool_own, ln1_var, ln1_sd, x_normed, tr1_done,
         proj_done, qk_out, v_out, scores_done, masked, max_done, shifted, exp_done, rcp_done, normed,
         p_turned, pT_out, pv_done, attn_out, abs_done, sums_done, tot_done, scale_done, w_int, w_quant,
         o_done, x2_out, x2_turned, mean_done, xc_done, ln2_var, ln2_sd, k_done, xi_done, xb_done, xq_turned,
         xq_out, d_diag, d_done, d_out, f1_done, f1_scaled, h_done, run_done, run_turned, se_diag, se_done,
         s_out, h_mul, h_int, hq_done, f2_done, y_scaled, y_added, gate_done) = (sem(n) for n in (
            "consts_made", "dve_own", "pool_own", "ln1_var", "ln1_sd", "x_normed", "tr1_done",
            "proj_done", "qk_out", "v_out", "scores_done", "masked", "max_done", "shifted",
            "exp_done", "rcp_done", "normed", "p_turned", "pT_out", "pv_done", "attn_out", "abs_done",
            "sums_done", "tot_done", "scale_done", "w_int", "w_quant", "o_done", "x2_out", "x2_turned",
            "mean_done", "xc_done", "ln2_var", "ln2_sd", "k_done", "xi_done", "xb_done", "xq_turned", "xq_out",
            "d_diag", "d_done", "d_out", "f1_done", "f1_scaled", "h_done", "run_done", "run_turned", "se_diag",
            "se_done", "s_out", "h_mul", "h_int", "hq_done", "f2_done", "y_scaled", "y_added", "gate_done"))

        MEAN_SLOT = 14
        SUM_W1 = (0, "S", 0)

        slot_units = {-2: [(0, "K", 0), (0, "K", 1), (0, "V", 0), (0, "V", 1)], -1: [(0, "Q", 0), (0, "Q", 1)]}
        for c in range(1, KC):
            s = 4 * (c - 1)
            slot_units[s] = [(c, "K", 0), (c, "K", 1)]
            slot_units[s + 1] = [(c, "Q", 0)]
            slot_units[s + 2] = [(c, "Q", 1)]
            slot_units[s + 3] = [(c, "V", 0), (c, "V", 1)]
        slot_units[MEAN_SLOT].append(SUM_W1)
        slot_units[4 * (KC - 1)] = slot_units.pop(4 * (KC - 1) - 2)
        unit_order = [u for s in sorted(slot_units) for u in slot_units[s]]
        NUMBER = {u: n for n, u in enumerate(unit_order)}
        reader = {"K": qk_out, "Q": qk_out, "V": v_out, "S": scale_done}
        COPIED = {u: sum(reader[v[1]] is reader[u[1]] for v in unit_order[:n + 1]) for n, u in enumerate(unit_order)}
        HEAD_START = {29: 0, 30: 1, 31: 2}

        def unit_copied(e, unit):
            e.wait_ge(reader[unit[1]], COPIED[unit])

        def projected(e, unit):
            e.wait_ge(proj_done, NUMBER[unit] + 1)

        job_slot = {4 * (c - 2): c for c in range(2, KC)} | {9 + 2 * o: KC + o for o in range(KC)}
        ORDER = [0, 1] + [job_slot[t] for t in sorted(job_slot)]
        AT = {job: n for n, job in enumerate(ORDER)}

        def job_data(job):
            if job < KC:
                return wq_raw[:, job % 2], wq_p[:, job % 2], wq_in[job % 2], 16 * (job // 2 + 1)
            o = job - KC
            return wout_raw[:, o % 3], wout_p[:, :, o], wout_in[o % 3], 16 * (o // 3 + 1)

        NT = 4 * NTILE
        FIRST_ROUND = MEAN_SLOT + 1
        FFN_SLOT = 44

        def slot_of(n):
            p, i = divmod(n, NTILE)
            return (2 * i // 5, FIRST_ROUND + 2 * i // 5, 28 + i // 2, FFN_SLOT + i)[p]

        tiles_of = {}
        for n in range(NT):
            tiles_of.setdefault(slot_of(n), []).append(n)
        LAST_SLOT = slot_of(NT - 1)

        def tiles_rounded(s):
            return [n // (2 * NTILE) * NTILE + n % NTILE for n in tiles_of.get(s, []) if n // NTILE % 2]

        def stage_wait(e, n):
            e.wait_ge(stage_in[n % NSTAGE], 16 * (n // NSTAGE + 1))

        def stage_free(e, n):
            m = n - NSTAGE
            if m < 0:
                return
            p, i = divmod(m, NTILE)
            if p % 2 == 0:
                e.wait_ge(abs_done, p // 2 * NTILE + i + 1)
            else:
                e.wait_ge(w_int, p // 2 * NTILE + i + 1)

        def quantised(e, t):
            e.wait_ge((w_quant, w_sign)[t % 2], t // 2 + 1)

        def all_quantised(e, w):
            quantised(e, NTILE * (w + 1) - 2)
            quantised(e, NTILE * (w + 1) - 1)

        def quantised_tile(t):
            w, i = divmod(t, NTILE)
            return w1_q[:, i] if w == 0 else w2_q[:, i // 4, i % 4 * KC:(i % 4 + 1) * KC]

        AT_BLOCK_PE = {1: [("x2", 4)], 3: [("x2", 5)], 5: [("x2", 6)], 7: [("x2", 7)], 14: [("xq", 4)],
                       15: [("xq", 5)], 17: [("xq", 6)], 19: [("xq", 7)], 20: [("d", 1)]}
        AT_BLOCK_DVE = {2: [("stats", 4)], 4: [("stats", 5), ("absmax", 4)], 6: [("stats", 6), ("absmax", 5)],
                        8: [("stats", 7), ("absmax", 6)], 9: [("absmax", 7), ("var", 1)], 11: [("scales", 1)],
                        13: [("cast", 4)], 14: [("cast", 5)], 16: [("cast", 6)], 18: [("cast", 7)]}
        AT_BLOCK_ACT = {2: [("centre", 4)], 4: [("centre", 5)], 6: [("centre", 6)], 8: [("centre", 7)],
                        10: [("root", 1)], 12: [("round", 4)], 13: [("round", 5)], 14: [("xq", 4)],
                        15: [("round", 6)], 16: [("xq", 5)], 17: [("round", 7)], 18: [("xq", 6)], 19: [("xq", 7)],
                        20: [("d", 1)]}

        block = ctx.enter_context(nc.Block())

        @block.sync
        def _(sp):
            def load_wq(c):
                if c >= 2:
                    sp.wait_ge(w_lo, AT[c - 2] + 1)
                sp.dma_start(wq_raw[:, c % 2], wq[c]).then_inc(wq_in[c % 2], 16)

            def load_wkv(c):
                if c >= 2:
                    projected(sp, (c - 2, "V", 1))
                sp.dma_start(wkv_sb[:, c % 2], wkv[c]).then_inc(wkv_in[c % 2], 16)

            def load_wout(o):
                if o >= 3:
                    sp.wait_ge(w_lo, AT[KC + o - 3] + 1)
                sp.dma_start(wout_raw[:, o % 3], wout[o]).then_inc(wout_in[o % 3], 16)

            def load_tile(n):
                p, i = divmod(n, NTILE)
                stage_free(sp, n)
                sp.dma_start(stage[:, n % NSTAGE, :], (w1, w2)[p // 2][i]).then_inc(stage_in[n % NSTAGE], 16)

            load_wkv(0)
            sp.dma_start(ctx_sb[:], ctx_t).then_inc(ctx_in, 16)
            for b in range(2):
                sp.dma_start(x_rows[:, b, :], x_tok[b]).then_inc(x_in[b], 16)
            load_wq(0)
            for b in range(2, B):
                sp.dma_start(x_rows[:, b, :], x_tok[b]).then_inc(x_in[b], 16)
            load_wq(1)
            load_wkv(1)
            sp.dma_start(wv_all, wv).then_inc(wv_in, 16)
            sp.dma_start(gates[:, 0:1], g_attn).then_inc(g_in, 16)
            sp.dma_start(gates[:, 1:2], g_ffn).then_inc(g_in, 16)
            for n in range(NSTAGE):
                load_tile(n)
            load_wq(2)
            load_wq(3)
            for s in range(LAST_SLOT + 1):
                c, i = s // 4 + 2, s % 4
                if i == 2 and c < KC:
                    load_wkv(c)
                if i == 1 and 4 <= c + 1 < KC:
                    load_wq(c + 1)
                if s >= 9 and s % 2 and (s - 9) // 2 < KC:
                    load_wout((s - 9) // 2)
                for n in tiles_of.get(s, []):
                    if n >= NSTAGE:
                        load_tile(n)
            for half in range(2):
                for o in range(KC):
                    u = KC * half + o
                    sp.wait_ge(y_added, u + 1)
                    sp.dma_start(out_t[o, :, half * HALF:(half + 1) * HALF], y_sb[:, u % 2, :])\
                        .then_inc(y_out[u % 2], 16)
            for r in range(2):
                sp.wait_ge(y_out[r], 16 * KC)

        @block.gpsimd
        def _(pool):
            pool.memset(ident[:], 0.0).then_inc(pool_own, 1)
            pool.memset(ident_b[:], 0.0).then_inc(pool_own, 1)
            pool.memset(mask[:], 0.0).then_inc(pool_own, 1)
            pool.memset(ones[:], 1.0).then_inc(consts_made, 1)
            pool.wait_ge(pool_own, 3)
            for m in (ident, ident_b):
                pool.affine_select(out=m[:], in_=m[:], compare_op=ALU.not_equal, fill=1.0, base=0,
                                   pattern=[[-1, P]], channel_multiplier=1).then_inc(consts_made, 1)
            pool.affine_select(out=mask[:], in_=mask[:], compare_op=ALU.is_ge, fill=NEG, base=0,
                               pattern=[[-1, S]], channel_multiplier=1).then_inc(consts_made, 1)

            def round_tile(n):
                p, i = divmod(n, NTILE)
                t = p // 2 * NTILE + i
                stage_wait(pool, n)
                if i == 0:
                    pool.wait_ge(scale_done, p // 2 + 1)
                if t >= NWI:
                    quantised(pool, t - NWI)
                nc.gpsimd.tensor_scalar(wint[:, t % NWI, :], stage[:, n % NSTAGE, :], wtot[:, p // 2, 2:3], 0.0,
                                        ALU.mult, ALU.add).then_inc(w_int, 1)

            def spread_max(job):
                n = AT[job]
                pool.wait_ge(wm_done, n + 1)
                nc.gpsimd.partition_all_reduce(wg[:, job:job + 1], wm[:, job:job + 1], P,
                                               bass.bass_isa.ReduceOp.max).then_inc(wg_done, 1)

            def ln1_norm(half):
                pool.wait_ge(ln1_ready, half + 1)
                for b in range(half * HB + 1, (half + 1) * HB, 2):
                    nc.gpsimd.tensor_scalar(x_rows[:, b, :], x_rows[:, b, :], tiny[:, 2, b:b + 1], tiny[:, 6, b:b + 1],
                                            ALU.mult, ALU.add).then_inc(x_normed_pool, 1)

            ln1_norm(0)
            spread_max(0)
            ln1_norm(1)
            spread_max(1)
            for s in range(LAST_SLOT + 1):
                if 1 <= s <= NGROUP:
                    g = s - 1
                    pool.wait_ge(rcp_done, g + 1)
                    nc.gpsimd.tensor_tensor(sm[:, g % NSM], sm[:, g % NSM],
                                            srcp[:, g % 2, :].to_broadcast([S, HB, S]), ALU.mult).then_inc(normed, 1)
                if s < NGROUP:
                    pool.wait_ge(max_done, s + 1)
                    nc.gpsimd.tensor_tensor(sm[:, s % NSM], sm[:, s % NSM],
                                            smax[:, s % 2, :].to_broadcast([S, HB, S]), ALU.subtract)\
                        .then_inc(shifted, 1)
                if s == 1:
                    pool.wait_ge(v_wm, 1)
                    nc.gpsimd.partition_all_reduce(wg[:, NJOB:NJOB + 2], wm[:, NJOB:NJOB + 2], P,
                                                   bass.bass_isa.ReduceOp.max).then_inc(v_wg, 1)
                if s in job_slot:
                    spread_max(job_slot[s])
                for n in tiles_of.get(s, []):
                    if n // NTILE % 2 == 1:
                        round_tile(n)
            for half in range(2):
                pool.wait_ge(s_out, half + 1)
                for j in range(FC):
                    q = half * FC + j
                    pool.wait_ge(h_done, q + 1)
                    h = h_ring[:, q % HSLOTS, :]
                    nc.gpsimd.tensor_tensor(h, h, s_bc, ALU.mult).then_inc(h_mul, 1)

        @block.scalar
        def _(act):
            def root(dst, src):
                return nc.scalar.activation(dst, src, ACT.Sqrt)

            def ln1_sums(b):
                act.wait_ge(x_in[b], 16)
                if b > 1:
                    act.wait_ge(ln1_act, b // 2)
                nc.scalar.activation(scratch, x_rows[:, b, :], ACT.Copy, accum_out=sums[:, 0, b:b + 1])\
                    .then_inc(act_own, 1)
                act.wait_ge(act_own, b // 2 * 2 + 1)
                nc.scalar.mul(tiny[:, 7, b:b + 1], sums[:, 0, b:b + 1], -1.0 / H).then_inc(act_own, 1)
                act.wait_ge(act_own, b // 2 * 2 + 2)
                nc.scalar.activation(scratch, x_rows[:, b, :], ACT.Square, bias=tiny[:, 7, b:b + 1],
                                     accum_out=sums[:, 1, b:b + 1]).then_inc(ln1_act, 1)

            def ln1_root(half):
                act.wait_ge(ln1_var, half + 1)
                root(tiny[:, 1, half * HB:(half + 1) * HB], tiny[:, 0, half * HB:(half + 1) * HB]).then_inc(ln1_sd, 1)

            def copy_xn(m):
                half, c = divmod(m, KC)
                act.wait_ge(tr1_done, m + 1)
                nc.scalar.copy(xn_T[:, 0, c, half * HALF:(half + 1) * HALF], bank[3 + m % 5][:, 0:HALF])\
                    .then_inc(xn_hi, 1)

            def split_hi(job):
                raw, pair, _, _ = job_data(job)
                act.wait_ge(ws_done, AT[job] + 1)
                if 2 <= job < KC:
                    projected(act, (job - 2, "Q", 1))
                nc.scalar.activation(pair[:, 0], raw, ACT.Copy, scale=ws[:, job:job + 1]).then_inc(w_hi, 1)

            def copy_unit(c, kind, half):
                projected(act, (c, kind, half))
                if c >= 2:
                    act.wait_ge(scores_done, 4 * (c - 1))
                src = bank[NUMBER[c, kind, half] % 3][:, 0:HALF]
                t = slice(half * HALF, (half + 1) * HALF)
                if kind == "K":
                    nc.scalar.copy(k_T[:, c % 2, t], src).then_inc(qk_out, 1)
                else:
                    nc.scalar.activation(q_T[:, c % 2, t], src, ACT.Copy, scale=wi[:, c:c + 1]).then_inc(qk_out, 1)

            def sign_tile(t):
                act.wait_ge(w_int, t + 1)
                nc.scalar.activation(quantised_tile(t), wint[:, t % NWI, :].rearrange("p (k m) -> p k m", k=KC),
                                     ACT.Sign, saturate=False).then_inc(w_sign, 1)

            def abs_tile(n):
                p, i = divmod(n, NTILE)
                stage_wait(act, n)
                w = stage[:, n % NSTAGE, :]
                if p // 2 * NTILE + i > 0:
                    act.wait_ge(abs_done, p // 2 * NTILE + i)
                nc.scalar.activation(w, w, ACT.Abs, accum_out=wsum[:, p // 2, i:i + 1]).then_inc(abs_done, 1)

            ln1_sums(1)
            ln1_sums(3)
            copy_unit(0, "K", 0)
            copy_unit(0, "K", 1)
            ln1_root(0)
            ln1_sums(5)
            for m in range(4):
                copy_xn(m)
            split_hi(0)
            ln1_sums(7)
            for m in range(4, KC):
                copy_xn(m)
            ln1_root(1)
            copy_unit(0, "Q", 0)
            for m in range(KC, 2 * KC):
                copy_xn(m)
            split_hi(1)
            copy_unit(0, "Q", 1)
            act.wait_ge(g_in, 32)
            nc.scalar.activation(gt[:], gates[:], ACT.Tanh).then_inc(gate_done, 1)
            for s in range(NGROUP + 3):
                for unit in slot_units.get(s, []):
                    if unit[1] in "KQ":
                        copy_unit(*unit)
                if s - 2 in job_slot:
                    split_hi(job_slot[s - 2])
                for n in tiles_of.get(s, []):
                    if n // NTILE % 2 == 0:
                        abs_tile(n)
                for t in tiles_rounded(s - 1):
                    if t % 2:
                        sign_tile(t)
                if 2 <= s < NGROUP + 2:
                    g = s - 2
                    act.wait_ge(p_turned, g + 1)
                    if g >= 2:
                        act.wait_ge(pv_done, g - 1)
                    nc.scalar.copy(pT[:, g % 2, :], bank[5 + g % 2][0:S, 0:HALF]).then_inc(pT_out, 1)
                if 4 <= s < NGROUP + 3 and s % 2 == 0:
                    q = (s - 4) // 2
                    act.wait_ge(pv_done, 2 * q + 2)
                    if q == 0:
                        act.wait_ge(v_ws, 1)
                    nc.scalar.activation(attn_T[:, 0, q // 2, (q % 2) * HALF:(q % 2 + 1) * HALF], bank[7][:, 0:HALF],
                                         ACT.Copy, scale=ws[:, NJOB:NJOB + 1]).then_inc(attn_out, 1)
                if s < NGROUP:
                    act.wait_ge(shifted, s + 1)
                    nc.scalar.activation(sm[:, s % NSM], sm[:, s % NSM], ACT.Exp).then_inc(exp_done, 1)
                if s == 29:
                    projected(act, (KC - 1, "Q", 1))
                    act.dma_start(x2_T, x_t).then_inc(xT_in, 16)

            def centre(n):
                act.wait_ge(mean_done, n + 1)
                if n == 0:
                    act.wait_ge(pv_done, NGROUP)
                if n == HB:
                    act.wait_ge(xi_done, HB)
                for t in range(2):
                    ins = nc.scalar.activation(xc_rows[:, n % HB, t * 512:(t + 1) * 512],
                                               bank[3 + 2 * (n % 2) + t][0:S, :], ACT.Identity,
                                               bias=tiny[:, 7, n:n + 1])
                ins.then_inc(xc_done, 1)

            def ln2_root(half):
                act.wait_ge(ln2_var, half + 1)
                hs = slice(half * HB, (half + 1) * HB)
                root(tiny[:, 1, hs], tiny[:, 0, hs]).then_inc(ln2_sd, 1)

            def round_x(n):
                act.wait_ge(k_done, n // HB + 1)
                if n >= 2:
                    act.wait_ge(xb_done, n - 1)
                nc.scalar.activation(xi_rows[:, n % 2, :], xc_rows[:, n % HB, :], ACT.Copy,
                                     scale=tiny[:, 5, n:n + 1]).then_inc(xi_done, 1)

            def copy_xq(n):
                act.wait_ge(xq_turned, n + 1)
                src = bank[7][:, 0:KC * S // 2].bitcast(BF16).rearrange("p (c t) -> p c t", c=KC)
                nc.scalar.copy(xq_T[:, :, n * S:(n + 1) * S], src).then_inc(xq_out, 1)

            def copy_d(half):
                act.wait_ge(d_done, half + 1)
                nc.scalar.copy(d_bc[:, half, :], bank[7][:, 0:HALF]).then_inc(d_out, 1)

            def gelu(half, j):
                q = half * FC + j
                act.wait_ge(f1_scaled, q + 1)
                if q >= HSLOTS:
                    act.wait_ge(h_int, q - HSLOTS + 1)
                elif q == 0:
                    act.wait_ge(o_done, 2 * KC)
                nc.scalar.activation(h_ring[:, q % HSLOTS, :], bank[q % 3][:, 0:HALF], ACT.Gelu).then_inc(h_done, 1)

            def round_h(q):
                act.wait_ge(h_mul, q + 1)
                if q == 0:
                    all_quantised(act, 1)
                if q >= 2:
                    act.wait_ge(hq_done, q - 1)
                nc.scalar.copy(hint[:, q % 2, :], h_ring[:, q % HSLOTS, :]).then_inc(h_int, 1)

            def copy_s(half):
                act.wait_ge(se_done, half + 1)
                if half == 0:
                    act.wait_ge(w_int, 2 * NTILE)
                else:
                    act.wait_ge(h_mul, FC)
                nc.scalar.copy(s_bc, bank[3][:, 0:HALF])
                nc.scalar.copy(e_bc[:, half, :], bank[4][:, 0:HALF]).then_inc(s_out, 1)

            for s in range(NGROUP + 3, FFN_SLOT):
                for n in tiles_of[s]:
                    abs_tile(n)
                if s >= FFN_SLOT - HB:
                    centre(s - FFN_SLOT + HB)
            ln2_root(0)
            round_x(0)
            for n in range(HB):
                if n + 1 < HB:
                    round_x(n + 1)
                copy_xq(n)
            copy_d(0)
            for j in range(FC):
                gelu(0, j)
                for step, n in AT_BLOCK_ACT.get(j, []):
                    (centre if step == "centre" else round_x if step == "round" else
                     copy_xq if step == "xq" else copy_d if step == "d" else ln2_root)(n)
                if j >= 4 and j % 2 == 0:
                    sign_tile(NTILE + j - 3)
            sign_tile(2 * NTILE - 3)
            sign_tile(2 * NTILE - 1)
            for j in range(FC):
                if j >= HG:
                    round_h(j - HG)
                gelu(1, j)
                if j == 3:
                    copy_s(0)
            for j in range(FC - HG, FC):
                round_h(j)
            copy_s(1)
            for j in range(FC):
                round_h(FC + j)

        @block.vector
        def _(dve):
            count = [0]

            def link(ins):
                count[0] += 1
                ins.then_inc(dve_own, 1)
                dve.wait_ge(dve_own, count[0])

            def inv_root(hs):
                ve, sd, r, t = (tiny[:, i, hs] for i in range(4))
                link(nc.vector.reciprocal(r, sd))
                link(nc.vector.tensor_tensor(t, r, r, ALU.mult))
                link(nc.vector.tensor_tensor(t, t, ve, ALU.mult))
                link(nc.vector.tensor_scalar(t, t, -0.5, 1.5, ALU.mult, ALU.add))
                link(nc.vector.tensor_tensor(r, r, t, ALU.mult))

            def largest(job):
                raw, _, arrived, value = job_data(job)
                dve.wait_ge(arrived, value)
                nc.vector.tensor_reduce(wm[:, job:job + 1], raw, AX.X, ALU.max, apply_absolute_value=True)\
                    .then_inc(wm_done, 1)

            def power_below(v):
                link(nc.vector.tensor_scalar(v, v, TINY, None, ALU.max))
                link(nc.vector.tensor_scalar(v.bitcast(I32), v.bitcast(I32), EXPONENT, None, ALU.bitwise_and))

            def scale(job):
                dve.wait_ge(wg_done, AT[job] + 1)
                g = wg[:, job:job + 1]
                power_below(g)
                link(nc.vector.reciprocal(ws[:, job:job + 1], g))
                if job < KC:
                    nc.vector.tensor_scalar(wi[:, job:job + 1], g, HD ** -0.5 / (TOP * XN_SCALE), None, ALU.mult)
                else:
                    if job == KC:
                        dve.wait_ge(gate_done, 1)
                    link(nc.vector.tensor_scalar(wi[:, job:job + 1], g, 1.0 / TOP, wi[:, NJOB:NJOB + 1],
                                                 ALU.mult, ALU.mult))
                    nc.vector.tensor_tensor(wi[:, job:job + 1], wi[:, job:job + 1], gt[:, 0:1], ALU.mult)
                nc.vector.tensor_scalar(ws[:, job:job + 1], ws[:, job:job + 1], TOP, None, ALU.mult).then_inc(ws_done, 1)

            def split_lo(job):
                raw, pair, _, _ = job_data(job)
                dve.wait_ge(w_hi, AT[job] + 1)
                nc.vector.scalar_tensor_tensor(pair[:, 1], raw, ws[:, job:job + 1], pair[:, 0],
                                               ALU.mult, ALU.subtract).then_inc(w_lo, 1)

            def v_magnitudes():
                dve.wait_ge(ctx_in, 16)
                dve.wait_ge(wv_in, 16)
                nc.vector.tensor_reduce(wm[:, NJOB:NJOB + 1], region_c[:], AX.X, ALU.max, apply_absolute_value=True)
                nc.vector.tensor_reduce(wm[:, NJOB + 1:NJOB + 2], wv_all, AX.X, ALU.max, apply_absolute_value=True)\
                    .then_inc(v_wm, 1)

            def attn_scale():
                dve.wait_ge(v_wg, 1)
                g = wg[:, NJOB:NJOB + 1]
                link(nc.vector.scalar_tensor_tensor(g, g, float(L), wg[:, NJOB + 1:NJOB + 2], ALU.mult, ALU.mult))
                power_below(g)
                link(nc.vector.reciprocal(ws[:, NJOB:NJOB + 1], g))
                nc.vector.tensor_scalar(wi[:, NJOB:NJOB + 1], g, 1.0 / TOP, None, ALU.mult)
                nc.vector.tensor_scalar(ws[:, NJOB:NJOB + 1], ws[:, NJOB:NJOB + 1], TOP, None, ALU.mult)\
                    .then_inc(v_ws, 1)

            def ln1_stats(b):
                dve.wait_ge(x_in[b], 16)
                for t in range(2):
                    last = nc.vector.bn_stats(bn[:, b, t, :], x_rows[:, b, t * 512:(t + 1) * 512])
                link(last)
                link(nc.vector.bn_aggr(mv[:, b, :], bn[:, b, :, :]))

            def ln1_norm(half):
                hs = slice(half * HB, (half + 1) * HB)
                even, odd = (slice(half * HB + i, (half + 1) * HB, 2) for i in range(2))
                nc.vector.tensor_scalar(tiny[:, 7, even], mv[:, even, 0], -1.0, None, ALU.mult)
                nc.vector.tensor_scalar(tiny[:, 0, even], mv[:, even, 1], LN_EPS, None, ALU.add)
                dve.wait_ge(ln1_act, HB // 2 * (half + 1))
                nc.vector.tensor_scalar(tiny[:, 0, odd], sums[:, 1, odd], 1.0 / H, LN_EPS, ALU.mult, ALU.add)\
                    .then_inc(ln1_var, 1)
                dve.wait_ge(ln1_sd, half + 1)
                inv_root(hs)
                link(nc.vector.tensor_scalar(tiny[:, 2, hs], tiny[:, 2, hs], XN_SCALE, None, ALU.mult))
                nc.vector.tensor_tensor(tiny[:, 6, hs], tiny[:, 7, hs], tiny[:, 2, hs], ALU.mult).then_inc(ln1_ready, 1)
                for b in range(half * HB, (half + 1) * HB, 2):
                    nc.vector.tensor_scalar(x_rows[:, b, :], x_rows[:, b, :], tiny[:, 7, b:b + 1], tiny[:, 2, b:b + 1],
                                            ALU.add, ALU.mult).then_inc(x_normed, 1)

            def xn_low(m):
                half, c = divmod(m, KC)
                t = slice(half * HALF, (half + 1) * HALF)
                dve.wait_ge(xn_hi, m + 1)
                nc.vector.tensor_tensor(xn_T[:, 1, c, t], bank[3 + m % 5][:, 0:HALF], xn_T[:, 0, c, t], ALU.subtract)\
                    .then_inc(xn_lo, 1)

            def copy_v(c, half):
                u = NUMBER[c, "V", half]
                projected(dve, (c, "V", half))
                if c >= 2:
                    dve.wait_ge(pv_done, 4 * (c - 1))
                nc.vector.tensor_copy(v_rows[:, c % 2, half * HB:(half + 1) * HB, :],
                                      bank[u % 3][0:S, :].rearrange("p (b f) -> p b f", b=HB)).then_inc(v_out, 1)

            def clip_tile(t):
                dve.wait_ge(w_int, t + 1)
                nc.vector.tensor_scalar(quantised_tile(t), wint[:, t % NWI, :].rearrange("p (k m) -> p k m", k=KC),
                                        1.0, -1.0, ALU.min, ALU.max, saturate=False).then_inc(w_quant, 1)

            def sum_columns(w):
                dve.wait_ge(abs_done, NTILE * (w + 1))
                nc.vector.tensor_reduce(wtot[:, w, 0:1], wsum[:, w, :], AX.X, ALU.add).then_inc(sums_done, 1)

            def finish_scale(w):
                if w == 0:
                    projected(dve, SUM_W1)
                else:
                    dve.wait_ge(tot_done, 1)
                src = bank[NUMBER[SUM_W1] % 3 if w == 0 else 7]
                link(nc.vector.tensor_scalar(wtot[:, w, 1:2], src[:, 0:1], 1.0 / (F * H), Q_EPS,
                                             ALU.mult, ALU.max))
                link(nc.vector.reciprocal(wtot[:, w, 2:3], wtot[:, w, 1:2]))
                nc.vector.tensor_scalar(wtot[:, w, 3:4], wtot[:, w, 1:2], 1.0 / Q_MAX, None, ALU.mult)\
                    .then_inc(scale_done, 1)

            ln1_stats(0)
            ln1_stats(2)
            ln1_norm(0)
            largest(0)
            copy_v(0, 0)
            copy_v(0, 1)
            ln1_stats(4)
            scale(0)
            for m in range(4):
                xn_low(m)
            ln1_stats(6)
            for m in range(4, KC):
                xn_low(m)
            split_lo(0)
            ln1_norm(1)
            largest(1)
            for m in range(KC, 2 * KC):
                xn_low(m)
            scale(1)
            split_lo(1)

            def attn_low(q):
                dve.wait_ge(attn_out, q + 1)
                c, t = q // 2, slice(q % 2 * HALF, (q % 2 + 1) * HALF)
                nc.vector.scalar_tensor_tensor(attn_T[:, 1, c, t], bank[7][:, 0:HALF], ws[:, NJOB:NJOB + 1],
                                               attn_T[:, 0, c, t], ALU.mult, ALU.subtract).then_inc(attn_lo, 1)

            def exp_sums(g):
                dve.wait_ge(exp_done, g + 1)
                link(nc.vector.tensor_reduce(ssum[:, g % 2, :], sm[:, g % NSM], AX.X, ALU.add))
                if g >= 2:
                    dve.wait_ge(normed, g - 1)
                nc.vector.reciprocal(srcp[:, g % 2, :], ssum[:, g % 2, :]).then_inc(rcp_done, 1)

            for s in range(NGROUP):
                if s:
                    exp_sums(s - 1)
                if s >= 5 and s % 2 == 1:
                    attn_low((s - 5) // 2)
                if s == MEAN_SLOT + 1:
                    finish_scale(0)
                for c, kind, half in slot_units.get(s, []):
                    if kind == "V":
                        copy_v(c, half)
                r = s % NSM
                dve.wait_ge(scores_done, s + 1)
                if s == 0:
                    dve.wait_ge(consts_made, 4)
                if s >= NSM:
                    dve.wait_ge(p_turned, s - NSM + 1)
                nc.vector.tensor_tensor(sm[:, r], bank[3 + s % 2][0:S, 0:HALF].rearrange("p (b k) -> p b k", b=HB),
                                        mask[:].unsqueeze(1).to_broadcast([S, HB, S]), ALU.add).then_inc(masked, 1)
                dve.wait_ge(masked, s + 1)
                if s >= 2:
                    dve.wait_ge(shifted, s - 1)
                nc.vector.tensor_reduce(smax[:, s % 2, :], sm[:, r], AX.X, ALU.max).then_inc(max_done, 1)
                if s == 0:
                    v_magnitudes()
                if s == 2:
                    attn_scale()
                if s in job_slot:
                    largest(job_slot[s])
                if s - 1 in job_slot:
                    scale(job_slot[s - 1])
                if s - 3 in job_slot:
                    split_lo(job_slot[s - 3])
                for t in tiles_rounded(s - 1):
                    if t % 2 == 0:
                        clip_tile(t)
                if s == MEAN_SLOT - 1:
                    sum_columns(0)
            exp_sums(NGROUP - 1)

            def gated_add(u):
                half, o = divmod(u, KC)
                dve.wait_ge(o_done, u + 1)
                if u == 0:
                    dve.wait_ge(xT_in, 16)
                x2 = x2_T[:, o, half * HALF:(half + 1) * HALF]
                nc.vector.scalar_tensor_tensor(x2, bank[u % 3][:, 0:HALF], wi[:, KC + o:KC + o + 1], x2,
                                               ALU.mult, ALU.add)\
                    .then_inc(x2_out, 1)

            def ln2_stats(n):
                dve.wait_ge(x2_turned, n + 1)
                for t in range(2):
                    last = nc.vector.bn_stats(bn[:, n, t, :], bank[3 + 2 * (n % 2) + t][0:S, :])
                link(last)
                link(nc.vector.bn_aggr(mv[:, n, :], bn[:, n, :, :]))
                nc.vector.tensor_scalar(tiny[:, 7, n:n + 1], mv[:, n, 0:1], -1.0, None, ALU.mult).then_inc(mean_done, 1)

            def ln2_absmax(n):
                dve.wait_ge(xc_done, n + 1)
                link(nc.vector.tensor_reduce(tiny[:, 4, n:n + 1], xc_rows[:, n % HB, :], AX.X, ALU.max,
                                             apply_absolute_value=True))

            def ln2_var_step(half):
                hs = slice(half * HB, (half + 1) * HB)
                nc.vector.tensor_scalar(tiny[:, 0, hs], mv[:, hs, 1], LN_EPS, None, ALU.add).then_inc(ln2_var, 1)

            def ln2_scales(half):
                hs = slice(half * HB, (half + 1) * HB)
                dve.wait_ge(ln2_sd, half + 1)
                inv_root(hs)
                r, t, am, k, d = (tiny[:, i, hs] for i in (2, 3, 4, 5, 6))
                link(nc.vector.tensor_tensor(am, am, r, ALU.mult))
                link(nc.vector.tensor_scalar(am, am, Q_EPS, None, ALU.max))
                link(nc.vector.reciprocal(t, am))
                nc.vector.scalar_tensor_tensor(k, t, Q_MAX, r, ALU.mult, ALU.mult).then_inc(k_done, 1)
                link(nc.vector.tensor_scalar(d, am, wtot[0:S, 0, 3:4], None, ALU.mult))
                if half:
                    dve.wait_ge(d_done, 1)
                spread(0, d).then_inc(d_diag, 1)

            def spread(r, v):
                return nc.vector.tensor_tensor(diag[:, r, :].rearrange("p (b k) -> p b k", b=HB),
                                               ident[0:S, 0:S].unsqueeze(1).to_broadcast([S, HB, S]),
                                               v.to_broadcast([S, HB, S]), ALU.mult)

            def cast_x(n):
                dve.wait_ge(xi_done, n + 1)
                if n >= 2:
                    dve.wait_ge(xq_turned, n - 1)
                nc.vector.tensor_copy(xb_rows[:, n % 2, :], xi_rows[:, n % 2, :]).then_inc(xb_done, 1)

            attn_low(2 * KC - 2)
            for u in range(2 * KC):
                if u == 3:
                    attn_low(2 * KC - 1)
                gated_add(u)
                o = u - KC
                if 1 <= o <= 4:
                    ln2_stats(o - 1)
                if 2 <= o <= 5:
                    ln2_absmax(o - 2)
                if o == 4:
                    ln2_var_step(0)
                if o == 5:
                    ln2_scales(0)
                    cast_x(0)
                    cast_x(1)
                if o == 6:
                    cast_x(2)
                if o == 7:
                    cast_x(3)
            sum_columns(1)

            def scale_block(q):
                dve.wait_ge(f1_done, q + 1)
                if q % FC == 0:
                    dve.wait_ge(d_out, q // FC + 1)
                nc.vector.tensor_tensor(bank[q % 3][:, 0:HALF], bank[q % 3][:, 0:HALF], d_bc[:, q // FC, :], ALU.mult)\
                    .then_inc(f1_scaled, 1)

            def run_max(g):
                dve.wait_ge(h_done, HG * (g + 1))
                r = HG * g % HSLOTS
                h = h_ring[:, r:r + HG, :].rearrange("p j t -> p t j")
                if g % (FC // HG) == 0:
                    if g:
                        dve.wait_ge(run_turned, 1)
                    nc.vector.tensor_reduce(run, h, AX.X, ALU.max, apply_absolute_value=True).then_inc(run_done, 1)
                else:
                    link(nc.vector.tensor_reduce(run4[:], h, AX.X, ALU.max, apply_absolute_value=True))
                    dve.wait_ge(run_done, g)
                    nc.vector.tensor_tensor(run, run, run4[:], ALU.max).then_inc(run_done, 1)

            def cast_h(q):
                dve.wait_ge(h_int, q + 1)
                half, j = divmod(q, FC)
                if q == 0:
                    dve.wait_ge(xq_turned, B)
                if q == FC:
                    dve.wait_ge(f1_done, 2 * FC)
                nc.vector.tensor_copy(hq[half][:, j, :], hint[:, q % 2, :]).then_inc(hq_done, 1)

            def h_scales(half):
                dve.wait_ge(run_turned, half + 1)
                am, s, e = (tiny[:, i, 0:HB] for i in (4, 5, 6))
                link(nc.vector.tensor_reduce(am, bank[3][0:S, :].rearrange("p (b f) -> p b f", b=HB), AX.X, ALU.max))
                link(nc.vector.tensor_scalar(am, am, Q_EPS, None, ALU.max))
                link(nc.vector.reciprocal(s, am))
                link(nc.vector.tensor_scalar(s, s, Q_MAX, None, ALU.mult))
                link(nc.vector.tensor_scalar(e, am, wtot[0:S, 1, 3:4], gt[0:S, 1:2], ALU.mult, ALU.mult))
                dve.wait_ge(d_done, 2)
                if half:
                    dve.wait_ge(se_done, 1)
                spread(0, s).then_inc(se_diag, 1)
                spread(1, e).then_inc(se_diag, 1)

            for q in range(2 * FC):
                scale_block(q)
                if q >= FC + HG + 1:
                    cast_h(q - FC - HG - 1)
                if q % HG == 0 and q:
                    run_max(q // HG - 1)
                for step, n in AT_BLOCK_DVE.get(q, []):
                    (ln2_stats if step == "stats" else ln2_absmax if step == "absmax" else
                     ln2_var_step if step == "var" else ln2_scales if step == "scales" else cast_x)(n)
                if q == 1:
                    finish_scale(1)
                if 3 <= q < FC + 3 and q % 2 == 1:
                    clip_tile(NTILE + q - 3)
                if q == FC + 2:
                    h_scales(0)
            cast_h(FC - HG - 1)
            run_max(2 * FC // HG - 1)
            for j in range(FC - 4, FC):
                cast_h(j)
            h_scales(1)
            for u in range(2 * KC):
                if u < KC:
                    for j in range(4 * u - 4, 4 * u) if u < KC - 1 else range(4 * u - 4, FC):
                        if j >= 0:
                            cast_h(FC + j)
                half, o = divmod(u, KC)
                dve.wait_ge(f2_done, u + 1)
                dve.wait_ge(s_out, half + 1)
                if u >= 2:
                    dve.wait_ge(y_out[u % 2], 16 * (u // 2))
                y = y_sb[:, u % 2, :]
                nc.vector.tensor_tensor(y, bank[(2 * FC + u) % 3][:, 0:HALF], e_bc[:, half, :], ALU.mult)\
                    .then_inc(y_scaled, 1)
                dve.wait_ge(y_scaled, u + 1)
                nc.vector.tensor_tensor(y, y, x2_T[:, o, half * HALF:(half + 1) * HALF], ALU.add).then_inc(y_added, 1)

        @block.tensor
        def _(pe):
            def turn_x(half):
                pe.wait_ge(consts_made, 4)
                pe.wait_ge(x_normed, HB // 2 * (half + 1))
                pe.wait_ge(x_normed_pool, HB // 2 * (half + 1))
                for c in range(KC):
                    m = half * KC + c
                    if m >= 5:
                        pe.wait_ge(xn_lo, m - 4)
                    for b in range(HB):
                        last = nc.tensor.transpose(bank[3 + m % 5][:, b * S:(b + 1) * S],
                                                   x_rows[:, half * HB + b, c * P:(c + 1) * P], ident[0:S, 0:S])
                    last.then_inc(tr1_done, 1)

            def split_product(out, w, x, ks, first, final):
                for k in ks:
                    wk = [w[:, p, k * P:(k + 1) * P] for p in range(2)]
                    xk = [x[:, p, k] for p in range(2)]
                    for n, (a, b) in enumerate(((0, 0), (0, 1), (1, 0))):
                        last = nc.tensor.matmul(out, wk[a], xk[b], start=(k == first and n == 0),
                                                stop=(k == final and n == 2))
                return last

            def project(c, kind, half):
                u = NUMBER[c, kind, half]
                if u >= 3:
                    unit_copied(pe, unit_order[u - 3])
                w = wkv_sb[:, c % 2]
                t = slice(half * HALF, (half + 1) * HALF)
                if kind in "KV":
                    pe.wait_ge(wkv_in[c % 2], 16 * (c // 2 + 1))
                    if c == 0:
                        pe.wait_ge(ctx_in, 16)
                if kind == "S":
                    last = total(0)
                elif kind == "K":
                    for k in range(LC):
                        last = nc.tensor.matmul(bank[u % 3][:, 0:HALF], w[:, k, :], ctx_sb[:, k, t],
                                                start=(k == 0), stop=(k == LC - 1))
                elif kind == "V":
                    for b in range(HB):
                        n = half * HB + b
                        for k in range(LC):
                            last = nc.tensor.matmul(bank[u % 3][0:S, b * P:(b + 1) * P],
                                                    ctx_sb[:, k, n * S:(n + 1) * S], w[:, LC + k, :],
                                                    start=(k == 0), stop=(k == LC - 1))
                else:
                    pe.wait_ge(w_lo, AT[c] + 1)
                    if c == 0:
                        pe.wait_ge(xn_lo, KC * (half + 1))
                    last = split_product(bank[u % 3][:, 0:HALF], wq_p[:, c % 2], xn_T[:, :, :, t], range(KC), 0, KC - 1)
                last.then_inc(proj_done, 1)

            def scores(g):
                c, half, h = g // 4, g // 2 % 2, g % 2
                unit_copied(pe, (c, "Q", half))
                unit_copied(pe, (c, "K", half))
                if g == 0:
                    pe.wait_ge(xn_lo, 2 * KC)
                if g >= 2:
                    pe.wait_ge(masked, g - 1)
                rows = slice(HD * h, HD * (h + 1))
                for b in range(HB):
                    t = slice((half * HB + b) * S, (half * HB + b + 1) * S)
                    last = nc.tensor.matmul(bank[3 + g % 2][0:S, b * S:(b + 1) * S], q_T[rows, c % 2, t],
                                            k_T[rows, c % 2, t], start=True, stop=True)
                last.then_inc(scores_done, 1)

            def turn_p(g):
                pe.wait_ge(normed, g + 1)
                if g >= 2:
                    pe.wait_ge(pT_out, g - 1)
                for b in range(HB):
                    last = nc.tensor.transpose(bank[5 + g % 2][0:S, b * S:(b + 1) * S], sm[:, g % NSM, b, :],
                                               ident[0:S, 0:S])
                last.then_inc(p_turned, 1)

            def weigh_v(g):
                c, half, h = g // 4, g // 2 % 2, g % 2
                pe.wait_ge(pT_out, g + 1)
                unit_copied(pe, (c, "V", half))
                if h == 0 and g:
                    pe.wait_ge(attn_lo, g // 2)
                for b in range(HB):
                    last = nc.tensor.matmul(bank[7][HD * h:HD * (h + 1), b * S:(b + 1) * S],
                                            v_rows[:, c % 2, half * HB + b, HD * h:HD * (h + 1)],
                                            pT[:, g % 2, b * S:(b + 1) * S], start=True, stop=True)
                last.then_inc(pv_done, 1)

            def total(w):
                pe.wait_ge(sums_done, w + 1)
                out = bank[NUMBER[SUM_W1] % 3 if w == 0 else 7]
                return nc.tensor.matmul(out[:, 0:1], ones[:], wtot[:, w, 0:1], start=True, stop=True)

            def out_proj(u, ks=range(KC)):
                half, o = divmod(u, KC)
                if 0 in ks:
                    pe.wait_ge(w_lo, NJOB)
                    if u < 3:
                        pe.wait_ge(v_out, 2 * KC)
                        pe.wait_ge(qk_out, 4 * KC)
                    else:
                        pe.wait_ge(x2_out, u - 2)
                pe.wait_ge(attn_lo, 2 * ks[-1] + 1 + half)
                last = split_product(bank[u % 3][:, 0:HALF], wout_p[:, :, o],
                                     attn_T[:, :, :, half * HALF:(half + 1) * HALF], ks, 0, KC - 1)
                if KC - 1 in ks:
                    last.then_inc(o_done, 1)

            def turn_x2(n):
                pe.wait_ge(x2_out, KC * (n // HB + 1))
                if n < 2:
                    pe.wait_ge((masked, pT_out)[n], NGROUP)
                else:
                    pe.wait_ge(xc_done, n - 1)
                for c in range(KC):
                    last = nc.tensor.transpose(bank[3 + 2 * (n % 2) + c // 4][0:S, c % 4 * P:(c % 4 + 1) * P],
                                               x2_T[:, c, n * S:(n + 1) * S], ident[:])
                last.then_inc(x2_turned, 1)

            def turn_xq(n):
                pe.wait_ge(xb_done, n + 1)
                if n == 0:
                    pe.wait_ge(attn_lo, 2 * KC)
                elif n == HB:
                    pe.wait_ge(scale_done, 2)
                else:
                    pe.wait_ge(xq_out, n)
                out = bank[7][:, 0:KC * S // 2].bitcast(BF16)
                for c in range(KC):
                    last = nc.tensor.transpose(out[:, c * S:(c + 1) * S], xb_rows[:, n % 2, c * P:(c + 1) * P],
                                               ident_b[0:S, 0:S])
                last.then_inc(xq_turned, 1)

            def spread_d(half):
                pe.wait_ge(d_diag, half + 1)
                pe.wait_ge(xq_out, HB * (half + 1))
                nc.tensor.matmul(bank[7][:, 0:HALF], ones[0:S, :], diag[:, 0, :], start=True, stop=True)\
                    .then_inc(d_done, 1)

            def hidden(q):
                half, j = divmod(q, FC)
                if q < 3:
                    pe.wait_ge(x2_out, 2 * KC)
                else:
                    pe.wait_ge(h_done, q - 2)
                if q == 0:
                    all_quantised(pe, 0)
                if j == 0:
                    pe.wait_ge(xq_out, HB * (half + 1))
                for k in range(KC):
                    last = nc.tensor.matmul(bank[q % 3][:, 0:HALF], w1_q[:, j, k, :],
                                            xq_T[:, k, half * HALF:(half + 1) * HALF],
                                            start=(k == 0), stop=(k == KC - 1))
                last.then_inc(f1_done, 1)

            def turn_run(half):
                pe.wait_ge(run_done, FC // HG * (half + 1))
                for b in range(HB):
                    last = nc.tensor.transpose(bank[3][0:S, b * P:(b + 1) * P], run[:, b * S:(b + 1) * S], ident[:])
                last.then_inc(run_turned, 1)

            def spread_se(half):
                pe.wait_ge(se_diag, 2 * half + 2)
                nc.tensor.matmul(bank[3][:, 0:HALF], ones[0:S, :], diag[:, 0, :], start=True, stop=True)
                nc.tensor.matmul(bank[4][:, 0:HALF], ones[0:S, :], diag[:, 1, :], start=True, stop=True)\
                    .then_inc(se_done, 1)

            def output(u):
                half, o = divmod(u, KC)
                q = 2 * FC + u
                if u < 3:
                    pe.wait_ge(h_done, q - 2)
                else:
                    pe.wait_ge(y_scaled, u - 2)
                if u == 0:
                    all_quantised(pe, 1)
                if o == 0:
                    pe.wait_ge(hq_done, FC * (half + 1))
                for k in range(FC):
                    last = nc.tensor.matmul(bank[q % 3][:, 0:HALF], w2_q[:, o, k, :], hq[half][:, k, :],
                                            start=(k == 0), stop=(k == FC - 1))
                    if u == 1 and k == KC:
                        spread_se(1)
                last.then_inc(f2_done, 1)

            for unit in slot_units[-2]:
                project(*unit)
            for half in range(2):
                turn_x(half)
                project(0, "Q", half)
            for s in range(NGROUP + 3):
                if s < NGROUP:
                    scores(s)
                for unit in slot_units.get(s, []):
                    project(*unit)
                if s in HEAD_START:
                    out_proj(HEAD_START[s], range(KC - 1))
                if 2 <= s < NGROUP + 2:
                    turn_p(s - 2)
                if s >= 3:
                    weigh_v(s - 3)
                if s == NGROUP + 1:
                    for u in range(3):
                        out_proj(u, range(KC - 1, KC))
                    out_proj(3)
            for u in range(4, 2 * KC):
                out_proj(u)
                o = u - KC
                if 0 <= o < HB:
                    turn_x2(o)
                if o in (6, 7):
                    turn_xq(2 * o - 12)
                    turn_xq(2 * o - 11)
            spread_d(0)
            for q in range(2 * FC):
                hidden(q)
                if q == 0:
                    pe.wait_ge(d_out, 1)
                    total(1).then_inc(tot_done, 1)
                for step, n in AT_BLOCK_PE.get(q, []):
                    (turn_x2 if step == "x2" else turn_xq if step == "xq" else spread_d)(n)
                if q == FC + 1:
                    turn_run(0)
                if q == FC + 3:
                    spread_se(0)
            for u in range(2 * KC):
                output(u)
                if u == 0:
                    turn_run(1)


def kernel(x, ctx_512, g_xattn, g_ffn, L0_xattn_Wq, L0_xattn_Wkv_expand, L0_xattn_Wout, L0_ffn_w1, L0_ffn_w2):
    import numpy as np
    import concourse.bacc as bacc
    from concourse.bass_utils import run_bass_kernel_spmd

    def a(v):
        return np.asarray(v)

    x, ctxs = a(x), a(ctx_512)

    def tiles(w):
        o, i = w.shape
        return w.reshape(o // P, P, i // P, P).transpose(0, 3, 2, 1)

    wkv = a(L0_xattn_Wkv_expand)
    arrays = {
        "x_tok": x,
        "x_t": x.reshape(N, KC, P).transpose(2, 1, 0),
        "ctx_t": ctxs[:, :S].reshape(N, LC, P).transpose(2, 1, 0),
        "wq": tiles(a(L0_xattn_Wq)).reshape(KC, P, H),
        "wkv": np.concatenate([tiles(wkv[:H]), tiles(wkv[H:])], axis=2),
        "wv": tiles(wkv[H:]).transpose(1, 0, 2, 3).reshape(P, LC * H),
        "wout": tiles(a(L0_xattn_Wout)).reshape(KC, P, H),
        "w1": tiles(a(L0_ffn_w1)),
        "w2": tiles(a(L0_ffn_w2)).reshape(KC, P, 4, KC * P).transpose(0, 2, 1, 3),
        "g_attn": np.broadcast_to(a(g_xattn).reshape(1, 1), (P, 1)),
        "g_ffn": np.broadcast_to(a(g_ffn).reshape(1, 1), (P, 1)),
    }
    arrays["w1"] = arrays["w1"].reshape(FC, P, H)
    arrays["w2"] = arrays["w2"].reshape(FC, P, H)
    arrays = {k: np.ascontiguousarray(v) for k, v in arrays.items()}
    nc = bacc.Bacc("TRN2", target_bir_lowering=False, num_devices=1, dynamic_dma_scratch_size=1024)
    aps = [nc.dram_tensor(k, v.shape, mybir.dt.from_np(v.dtype), kind="ExternalInput").ap() for k, v in arrays.items()]
    out = nc.dram_tensor("out_t", (KC, P, N), F32, kind="ExternalOutput").ap()
    flamingo_layer(nc, *aps, out)
    r = run_bass_kernel_spmd(nc, [arrays], core_ids=[0])
    got = r.results[0]["out_t"]
    return np.ascontiguousarray(got.reshape(H, N).T).reshape(B, S, H)
```

```python
from contextlib import ExitStack

import concourse.bass as bass
from concourse import mybir

F32 = mybir.dt.float32
BF16 = mybir.dt.bfloat16
F8 = mybir.dt.float8e4
F16 = mybir.dt.float16
I16 = mybir.dt.int16
I32 = mybir.dt.int32
ALU = mybir.AluOpType
ACT = mybir.ActivationFunctionType
AX = mybir.AxisListType

P = 128
B, S, H = 8, 100, 1024
L = 256
HD = 64
F = 4096
N = B * S
HALF = N // 2
HB = B // 2
KC = H // P
LC = L // P
FC = F // P
LN_EPS = 1e-5
Q_EPS = 1e-5
Q_MAX = 127.0
NEG = -3.0e38
TINY = 1e-30
EXPONENT = 0x7F800000
TOP = 2.0 ** 14
XN_SCALE = 2.0 ** 10

NSTAGE = 4
NTILE = FC
NWI = 4
NJOB = 2 * KC
HG = 4
HSLOTS = FC + HG
LAG = 7
NGROUP = 4 * KC


def flamingo_layer(nc, x_tok, x_t, ctx_t, wq, wkv, wv, wout, w1, w2, g_attn, g_ffn, out_t):
    with ExitStack() as ctx:
        def sb(name, shape, dt):
            return ctx.enter_context(nc.sbuf_tensor(name, shape, dt))

        def sem(name):
            return ctx.enter_context(nc.semaphore(name))

        def sems(names):
            return [sem(name) for name in names.split()]

        region_x = sb("region_x", [P, KC * N], F32)
        xn_T = region_x[:].bitcast(F16).rearrange("p (s c t) -> p s c t", s=2, c=KC)
        x2_T = region_x[:].rearrange("p (c t) -> p c t", c=KC)
        region_aw = sb("region_aw", [P, max(KC * N + KC * H, HSLOTS * HALF)], F32)
        attn_T = region_aw[:, 0:KC * N].bitcast(F16).rearrange("p (s c t) -> p s c t", s=2, c=KC)
        wout_p = region_aw[:, KC * N:KC * N + KC * H].bitcast(F16).rearrange("p (s o f) -> p s o f", s=2, o=KC)
        wv_all = region_aw[:, 0:LC * H]
        h_ring = region_aw[:, 0:HSLOTS * HALF].rearrange("p (s t) -> p s t", s=HSLOTS)
        region_w1 = sb("region_w1", [P, B * H], F32)
        x_rows = region_w1[0:S, :].rearrange("p (b f) -> p b f", b=B)
        w1_q = region_w1[:].bitcast(F8).rearrange("p (j k m) -> p j k m", j=FC, k=KC)
        hq_b = region_w1[:, 0:FC * HALF // 2].bitcast(BF16).rearrange("p (j t) -> p j t", j=FC)
        region_w2 = sb("region_w2", [P, B * H], F32)
        wq_raw = region_w2[:, 0:2 * H].rearrange("p (r f) -> p r f", r=2)
        wkv_sb = region_w2[:, 2 * H:3 * H].rearrange("p (r k m) -> p r k m", r=2, m=P)
        wq_p = region_w2[:, 3 * H:5 * H].bitcast(F16).rearrange("p (r s f) -> p r s f", r=2, s=2)
        wout_raw = region_w2[:, 5 * H:8 * H].rearrange("p (r f) -> p r f", r=3)
        w2_q = region_w2[:].bitcast(F8).rearrange("p (o k m) -> p o k m", o=KC, k=FC)
        region_h = sb("region_h", [P, FC * HALF // 2], F32)
        q_T = region_h[:, 0:2 * N].rearrange("p (r t) -> p r t", r=2)
        k_T = region_h[:, 2 * N:4 * N].rearrange("p (r t) -> p r t", r=2)
        v_rows = region_h[0:S, 4 * N:4 * N + 2 * B * P].rearrange("p (r b f) -> p r b f", r=2, b=B)
        xc_rows = region_h[0:S, 0:HB * H].rearrange("p (b f) -> p b f", b=HB)
        xi_rows = region_h[0:S, HB * H:HB * H + H].bitcast(I16).rearrange("p (r f) -> p r f", r=2)
        xb_rows = region_h[0:S, HB * H + H:HB * H + 2 * H].bitcast(BF16).rearrange("p (r f) -> p r f", r=2)
        hq_a = region_h[:].bitcast(BF16).rearrange("p (j t) -> p j t", j=FC)
        hq = [hq_a, hq_b]
        NSM = 4
        region_q = sb("region_q", [P, KC * N // 2], F32)
        sm = region_q[0:S, 0:NSM * HALF].rearrange("p (r b k) -> p r b k", r=NSM, b=HB)
        pT = region_q[0:S, NSM * HALF:(NSM + 2) * HALF].rearrange("p (r t) -> p r t", r=2)
        xq_T = region_q[:].bitcast(BF16).rearrange("p (c t) -> p c t", c=KC)
        region_c = sb("region_c", [P, LC * N], F32)
        ctx_sb = region_c[:].rearrange("p (c t) -> p c t", c=LC)
        d_bc = region_c[:, 0:N].rearrange("p (r t) -> p r t", r=2)
        s_bc = region_c[:, N:N + HALF]
        run = region_c[:, N + HALF:N + 2 * HALF]
        stage = sb("stage", [P, NSTAGE, H], F32)
        h_more = stage[:, 1:3, :].rearrange("p r m -> p (r m)")[:, 0:HG * HALF].rearrange("p (s t) -> p s t", s=HG)
        e_bc = stage[:, 0, 0:2 * HALF].rearrange("p (r t) -> p r t", r=2)
        region_i = sb("region_i", [P, NWI * H], I16)
        wint = region_i[:].rearrange("p (r m) -> p r m", r=NWI)
        hint = region_i[:, 0:2 * HALF].rearrange("p (r t) -> p r t", r=2)
        y_sb = region_i[:, 2 * HALF:6 * HALF].bitcast(F32).rearrange("p (r t) -> p r t", r=2)
        run4 = sb("run4", [P, HALF], F32)
        diag = sb("diag", [S, 2, HALF], F32)
        ident = sb("ident", [P, P], F32)
        ident_b = sb("ident_b", [P, P], BF16)
        ones = sb("ones", [P, P], F32)
        mask = sb("mask", [S, S], BF16)
        bn = sb("bn", [S, B, 2, 6], F32)
        mv = sb("mv", [S, B, 2], F32)
        sums = sb("sums", [S, 2, B], F32)
        scratch = region_aw[0:S, LC * H:LC * H + H]
        tiny = sb("tiny", [S, 8, B], F32)
        minus_half = sb("minus_half", [S, HB], F32)
        smax = sb("smax", [S, 2, HB], F32)
        ssum = sb("ssum", [S, 2, HB], F32)
        srcp = sb("srcp", [S, 2, HB], F32)
        gates = sb("gates", [P, 2], F32)
        gt = sb("gt", [P, 2], F32)
        wsum = sb("wsum", [P, 2, NTILE], F32)
        wtot = sb("wtot", [P, 2, 4], F32)
        wm = sb("wm", [P, NJOB + 2], F32)
        wg = sb("wg", [P, NJOB + 2], F32)
        ws = sb("ws", [P, NJOB + 1], F32)
        wi = sb("wi", [P, NJOB + 1], F32)
        bank = [ctx.enter_context(nc.psum_tensor(f"bank{i}", [P, 512], F32)) for i in range(8)]

        x_in = [sem(f"x_in{b}") for b in range(B)]
        ctx_in, g_in = (sem(n) for n in ("ctx_in", "g_in"))
        xT_in = [sem(f"xT_in{r}") for r in range(4)]
        y_out = [sem(f"y_out{r}") for r in range(2)]
        wq_in = [sem(f"wq_in{r}") for r in range(2)]
        wkv_in = [sem(f"wkv_in{r}") for r in range(2)]
        wout_in = [sem(f"wout_in{r}") for r in range(3)]
        stage_in = [sem(f"stage_in{r}") for r in range(NSTAGE)]
        consts_made, dve_own, pool_own, act_own, gate_done = sems("consts_made dve_own pool_own act_own gate_done")
        ln1_act, ln1_var, ln1_sd, ln1_ready, x_normed = sems("ln1_act ln1_var ln1_sd ln1_ready x_normed")
        x_normed_pool, tr1_done, xn_hi, xn_lo = sems("x_normed_pool tr1_done xn_hi xn_lo")
        wv_in, v_wm, v_wg, v_ws, wm_done, wg_done, ws_done = sems("wv_in v_wm v_wg v_ws wm_done wg_done ws_done")
        w_hi, w_lo = sems("w_hi w_lo")
        proj_done, qk_out, v_out, scores_done, max_done = sems("proj_done qk_out v_out scores_done max_done")
        exp_done, rcp_done, normed, p_turned, pT_out, pv_done = sems("exp_done rcp_done normed p_turned pT_out pv_done")
        attn_out, attn_lo = sems("attn_out attn_lo")
        abs_done, sums_done, tot_done, scale_done, w_int = sems("abs_done sums_done tot_done scale_done w_int")
        w_quant, w_sign = sems("w_quant w_sign")
        o_done, x2_out, x2_turned, mean_done, xc_done = sems("o_done x2_out x2_turned mean_done xc_done")
        ln2_var, ln2_root, k_done, xi_done, xb_done = sems("ln2_var ln2_root k_done xi_done xb_done")
        xq_turned, xq_out, d_diag, d_done, d_out = sems("xq_turned xq_out d_diag d_done d_out")
        f1_done, f1_scaled, h_done, run_done, run_turned = sems("f1_done f1_scaled h_done run_done run_turned")
        se_diag, se_done, s_out, h_mul, h_int, hq_done = sems("se_diag se_done s_out h_mul h_int hq_done")
        f2_done, y_scaled, y_added = sems("f2_done y_scaled y_added")

        MEAN_SLOT = 14
        SUM_W1 = (0, "S", 0)

        slot_units = {-2: [(0, "K", 0), (0, "K", 1), (0, "V", 0), (0, "V", 1)], -1: [(0, "Q", 0), (0, "Q", 1)]}
        for c in range(1, KC):
            s = 4 * (c - 1)
            slot_units[s] = [(c, "K", 0), (c, "K", 1)]
            slot_units[s + 1] = [(c, "Q", 0)]
            slot_units[s + 2] = [(c, "Q", 1)]
            slot_units[s + 3] = [(c, "V", 0), (c, "V", 1)]
        slot_units[MEAN_SLOT].append(SUM_W1)
        slot_units[4 * (KC - 1)] = slot_units.pop(4 * (KC - 1) - 2)
        slot_units[4 * (KC - 1) - 2] = slot_units.pop(4 * (KC - 1) - 3)
        part_of_q = {}
        for c in range(1, KC):
            s = 4 * (c - 1)
            part_of_q[s, (c, "Q", 0)] = range(2)
            if c < KC - 1:
                part_of_q[s + 1, (c, "Q", 0)] = range(2, KC)
                part_of_q[s + 1, (c, "Q", 1)] = range(1)
                part_of_q[s + 2, (c, "Q", 1)] = range(1, KC)
            else:
                part_of_q[s + 1, (c, "Q", 0)] = range(2, 5)
                part_of_q[s + 2, (c, "Q", 0)] = range(5, KC)
        unit_order = [u for s in sorted(slot_units) for u in slot_units[s]]
        NUMBER = {u: n for n, u in enumerate(unit_order)}
        reader = {"K": qk_out, "Q": qk_out, "V": v_out, "S": scale_done}
        COPIED = {u: sum(reader[v[1]] is reader[u[1]] for v in unit_order[:n + 1]) for n, u in enumerate(unit_order)}
        HEAD_START = {29: 0, 30: 1, 31: 2}

        def unit_copied(e, unit):
            e.wait_ge(reader[unit[1]], COPIED[unit])

        def projected(e, unit):
            e.wait_ge(proj_done, NUMBER[unit] + 1)

        job_slot = {4 * (c - 2): c for c in range(2, KC)} | {9 + 2 * o: KC + o for o in range(KC)}
        ORDER = [0, 1] + [job_slot[t] for t in sorted(job_slot)]
        AT = {job: n for n, job in enumerate(ORDER)}

        def job_data(job):
            if job < KC:
                return wq_raw[:, job % 2], wq_p[:, job % 2], wq_in[job % 2], 16 * (job // 2 + 1)
            o = job - KC
            return wout_raw[:, o % 3], wout_p[:, :, o], wout_in[o % 3], 16 * (o // 3 + 1)

        NT = 4 * NTILE
        FIRST_ROUND = MEAN_SLOT + 1
        FFN_SLOT = 47

        def slot_of(n):
            p, k = divmod(n, NTILE)
            if p == 2:
                return 28 + k // 2 if k < 4 else 26 + k if k < 8 else 34 + (k - 8) * 10 // 24
            if p == 3:
                return FFN_SLOT - 2 + k // 2 if k < NSTAGE else FFN_SLOT + k - NSTAGE
            return (2 * k // 5, FIRST_ROUND + 2 * k // 5)[p]

        LOADS = (0, NTILE, 2 * NTILE - NSTAGE, 3 * NTILE - NSTAGE)

        def load_of(n):
            p, k = divmod(n, NTILE)
            return LOADS[p] + k - (NSTAGE if p % 2 else 0)

        def tile_of(k):
            return (k - NSTAGE) % NTILE

        tiles_of = {}
        for n in range(NT):
            tiles_of.setdefault(slot_of(n), []).append(n)
        LAST_SLOT = slot_of(NT - 1)

        def tiles_rounded(s):
            return [n // (2 * NTILE) * NTILE + n % NTILE for n in tiles_of.get(s, []) if n // NTILE % 2]

        def stage_tile(n):
            return stage[:, load_of(n) % NSTAGE, :]

        def stage_wait(e, n):
            e.wait_ge(stage_in[load_of(n) % NSTAGE], 16 * (load_of(n) // NSTAGE + 1))

        def stage_free(e, n):
            load = load_of(n) - NSTAGE
            if load < 0:
                return
            w, i = divmod(load, 2 * NTILE - NSTAGE)
            if i < NTILE - NSTAGE:
                e.wait_ge(abs_done, w * NTILE + i + 1)
            else:
                e.wait_ge(w_int, w * NTILE + i - (NTILE - NSTAGE) + 1)

        def by_dve(t):
            return t % 2 == 0 and not NTILE + NSTAGE <= t < NTILE + 24

        def quantised(e, t):
            e.wait_ge(w_quant if by_dve(t) else w_sign, sum(by_dve(v) == by_dve(t) for v in range(t + 1)))

        def all_quantised(e, w):
            last = NTILE * (w + 1) - 1
            quantised(e, last)
            quantised(e, max(t for t in range(last) if by_dve(t) != by_dve(last)))

        def quantised_tile(t):
            w, k = divmod(t, NTILE)
            i = tile_of(k)
            return w1_q[:, i] if w == 0 else w2_q[:, i // 4, i % 4 * KC:(i % 4 + 1) * KC]

        AT_OUTPUT_DVE = {8: [("stats", 0)], 9: [("stats", 1), ("absmax", 0)], 10: [("stats", 2), ("absmax", 1)],
                         11: [("stats", 3), ("var", 0), ("absmax", 2)], 12: [("absmax", 3), ("scales", 0)],
                         13: [("sum", 1)]}
        AT_BLOCK_PE = {1: [("x2", 4)], 5: [("x2", 5)], 9: [("x2", 6)], 14: [("x2", 7)],
                       23: [("xq", 4)], 25: [("xq", 5)], 27: [("xq", 6)], 29: [("xq", 7)], 31: [("d", 1)]}
        AT_BLOCK_DVE = {2: [("stats", 4)], 5: [("absmax", 4)], 6: [("stats", 5)], 9: [("absmax", 5)],
                        10: [("stats", 6)], 13: [("absmax", 6)], 15: [("stats", 7), ("var", 1)], 17: [("absmax", 7)],
                        18: [("scales", 1)], 19: [("cast", 4)], 21: [("cast", 5)], 23: [("cast", 6)],
                        25: [("cast", 7)]}
        AT_BLOCK_ACT = {3: [("centre", 4)], 7: [("centre", 5)], 11: [("centre", 6)], 15: [("centre", 7)],
                        18: [("round", 4)], 20: [("round", 5)], 22: [("round", 6)], 23: [("xq", 4)],
                        24: [("round", 7)], 25: [("xq", 5)], 27: [("xq", 6)], 29: [("xq", 7)], 31: [("d", 1)]}

        def h_slots(q, count=1):
            r = q % (HSLOTS + HG)
            return h_ring[:, r:r + count, :] if r < HSLOTS else h_more[:, r - HSLOTS:r - HSLOTS + count, :]

        block = ctx.enter_context(nc.Block())

        @block.sync
        def _(sp):
            def load_wq(c):
                if c >= 2:
                    sp.wait_ge(w_lo, AT[c - 2] + 1)
                sp.dma_start(wq_raw[:, c % 2], wq[c]).then_inc(wq_in[c % 2], 16)

            def load_wkv(c):
                if c >= 2:
                    projected(sp, (c - 2, "V", 1))
                sp.dma_start(wkv_sb[:, c % 2], wkv[c]).then_inc(wkv_in[c % 2], 16)

            def load_wout(o):
                if o >= 3:
                    sp.wait_ge(w_lo, AT[KC + o - 3] + 1)
                sp.dma_start(wout_raw[:, o % 3], wout[o]).then_inc(wout_in[o % 3], 16)

            def load_tile(n):
                p, k = divmod(n, NTILE)
                if p % 2 and k < NSTAGE:
                    return
                stage_free(sp, n)
                sp.dma_start(stage_tile(n), (w1, w2)[p // 2][tile_of(k) if p % 2 else k])\
                    .then_inc(stage_in[load_of(n) % NSTAGE], 16)

            for b in range(4):
                sp.dma_start(x_rows[:, b, :], x_tok[b]).then_inc(x_in[b], 16)
            load_wq(0)
            load_wkv(0)
            sp.dma_start(ctx_sb[:], ctx_t).then_inc(ctx_in, 16)
            for b in range(4, B):
                sp.dma_start(x_rows[:, b, :], x_tok[b]).then_inc(x_in[b], 16)
            load_wq(1)
            load_wkv(1)
            sp.dma_start(wv_all, wv).then_inc(wv_in, 16)
            sp.dma_start(gates[:, 0:1], g_attn).then_inc(g_in, 16)
            sp.dma_start(gates[:, 1:2], g_ffn).then_inc(g_in, 16)
            for n in range(NSTAGE):
                load_tile(n)
            load_wq(2)
            load_wq(3)
            for s in range(LAST_SLOT + 1):
                c, i = s // 4 + 2, s % 4
                if i == 2 and c < KC:
                    load_wkv(c)
                if i == 1 and 4 <= c + 1 < KC:
                    load_wq(c + 1)
                if s >= 9 and s % 2 and (s - 9) // 2 < KC:
                    load_wout((s - 9) // 2)
                if 30 <= s < 34:
                    r = s - 30
                    projected(sp, (KC - 1, "Q", 1))
                    sp.dma_start(x2_T[:, 2 * r:2 * r + 2], x_t[:, 2 * r:2 * r + 2]).then_inc(xT_in[r], 16)
                for n in tiles_of.get(s, []):
                    if n >= NSTAGE:
                        load_tile(n)
            for half in range(2):
                for o in range(KC):
                    u = KC * half + o
                    sp.wait_ge(y_added, u + 1)
                    sp.dma_start(out_t[o, :, half * HALF:(half + 1) * HALF], y_sb[:, u % 2, :])\
                        .then_inc(y_out[u % 2], 16)
            for r in range(2):
                sp.wait_ge(y_out[r], 16 * KC)

        @block.gpsimd
        def _(pool):
            pool.memset(ident[:], 0.0).then_inc(pool_own, 1)
            pool.memset(ident_b[:], 0.0).then_inc(pool_own, 1)
            pool.memset(mask[:], 0.0).then_inc(pool_own, 1)
            pool.memset(minus_half[:], -0.5).then_inc(pool_own, 1)
            pool.memset(ones[:], 1.0).then_inc(consts_made, 1)
            pool.wait_ge(pool_own, 4)
            for m in (ident, ident_b):
                pool.affine_select(out=m[:], in_=m[:], compare_op=ALU.not_equal, fill=1.0, base=0,
                                   pattern=[[-1, P]], channel_multiplier=1).then_inc(consts_made, 1)
            pool.affine_select(out=mask[:], in_=mask[:], compare_op=ALU.is_ge, fill=NEG, base=0,
                               pattern=[[-1, S]], channel_multiplier=1).then_inc(consts_made, 1)

            def round_tile(n):
                p, i = divmod(n, NTILE)
                t = p // 2 * NTILE + i
                stage_wait(pool, n)
                if i == 0:
                    pool.wait_ge(scale_done, p // 2 + 1)
                if t >= NWI:
                    quantised(pool, t - NWI)
                nc.gpsimd.tensor_scalar(wint[:, t % NWI, :], stage_tile(n), wtot[:, p // 2, 2:3], 0.0,
                                        ALU.mult, ALU.add).then_inc(w_int, 1)

            def spread_max(job):
                n = AT[job]
                pool.wait_ge(wm_done, n + 1)
                nc.gpsimd.partition_all_reduce(wg[:, job:job + 1], wm[:, job:job + 1], P,
                                               bass.bass_isa.ReduceOp.max).then_inc(wg_done, 1)

            def inverse_root(half, var, done):
                hs = slice(half * HB, (half + 1) * HB)
                pool.wait_ge(var, half + 1)
                nc.gpsimd.tensor_tensor(tiny[:, 2, hs], tiny[:, 0, hs], minus_half[:], ALU.pow).then_inc(done, 1)

            def ln1_norm(half):
                pool.wait_ge(ln1_ready, half + 1)
                for b in range(half * HB + 1, (half + 1) * HB, 2):
                    nc.gpsimd.tensor_scalar(x_rows[:, b, :], x_rows[:, b, :], tiny[:, 2, b:b + 1], tiny[:, 6, b:b + 1],
                                            ALU.mult, ALU.add).then_inc(x_normed_pool, 1)

            ln1_norm(0)
            spread_max(0)
            ln1_norm(1)
            spread_max(1)
            for s in range(LAST_SLOT + 1):
                if 1 <= s <= NGROUP:
                    g = s - 1
                    pool.wait_ge(rcp_done, g + 1)
                    nc.gpsimd.tensor_tensor(sm[:, g % NSM], sm[:, g % NSM],
                                            srcp[:, g % 2, :].to_broadcast([S, HB, S]), ALU.mult).then_inc(normed, 1)
                if s == 1:
                    pool.wait_ge(v_wm, 1)
                    nc.gpsimd.partition_all_reduce(wg[:, NJOB:NJOB + 2], wm[:, NJOB:NJOB + 2], P,
                                                   bass.bass_isa.ReduceOp.max).then_inc(v_wg, 1)
                if s in job_slot:
                    spread_max(job_slot[s])
                if s in (FFN_SLOT - 4, FFN_SLOT + 17):
                    inverse_root(s // FFN_SLOT, ln2_var, ln2_root)
                for n in tiles_of.get(s, []):
                    if n // NTILE % 2 == 1:
                        round_tile(n)
            for half in range(2):
                pool.wait_ge(s_out, half + 1)
                for j in range(FC):
                    q = half * FC + j
                    pool.wait_ge(h_done, q + 1)
                    h = h_slots(q)[:, 0]
                    nc.gpsimd.tensor_tensor(h, h, s_bc, ALU.mult).then_inc(h_mul, 1)

        @block.scalar
        def _(act):
            def root(dst, src):
                return nc.scalar.activation(dst, src, ACT.Sqrt)

            def ln1_sums(b):
                act.wait_ge(x_in[b], 16)
                if b > 1:
                    act.wait_ge(ln1_act, b // 2)
                nc.scalar.activation(scratch, x_rows[:, b, :], ACT.Copy, accum_out=sums[:, 0, b:b + 1])\
                    .then_inc(act_own, 1)
                act.wait_ge(act_own, b // 2 * 2 + 1)
                nc.scalar.mul(tiny[:, 7, b:b + 1], sums[:, 0, b:b + 1], -1.0 / H).then_inc(act_own, 1)
                act.wait_ge(act_own, b // 2 * 2 + 2)
                nc.scalar.activation(scratch, x_rows[:, b, :], ACT.Square, bias=tiny[:, 7, b:b + 1],
                                     accum_out=sums[:, 1, b:b + 1]).then_inc(ln1_act, 1)

            def ln1_root(half):
                act.wait_ge(ln1_var, half + 1)
                root(tiny[:, 1, half * HB:(half + 1) * HB], tiny[:, 0, half * HB:(half + 1) * HB]).then_inc(ln1_sd, 1)

            def copy_xn(m):
                half, c = divmod(m, KC)
                act.wait_ge(tr1_done, m + 1)
                nc.scalar.copy(xn_T[:, 0, c, half * HALF:(half + 1) * HALF], bank[3 + m % 5][:, 0:HALF])\
                    .then_inc(xn_hi, 1)

            def split_hi(job):
                raw, pair, _, _ = job_data(job)
                act.wait_ge(ws_done, AT[job] + 1)
                if 2 <= job < KC:
                    projected(act, (job - 2, "Q", 1))
                nc.scalar.activation(pair[:, 0], raw, ACT.Copy, scale=ws[:, job:job + 1]).then_inc(w_hi, 1)

            def copy_unit(c, kind, half):
                projected(act, (c, kind, half))
                if c >= 2:
                    act.wait_ge(scores_done, 4 * (c - 1))
                src = bank[NUMBER[c, kind, half] % 3][:, 0:HALF]
                t = slice(half * HALF, (half + 1) * HALF)
                if kind == "K":
                    nc.scalar.copy(k_T[:, c % 2, t], src).then_inc(qk_out, 1)
                else:
                    nc.scalar.activation(q_T[:, c % 2, t], src, ACT.Copy, scale=wi[:, c:c + 1]).then_inc(qk_out, 1)

            def sign_tile(t):
                act.wait_ge(w_int, t + 1)
                nc.scalar.activation(quantised_tile(t), wint[:, t % NWI, :].rearrange("p (k m) -> p k m", k=KC),
                                     ACT.Sign, saturate=False).then_inc(w_sign, 1)

            def abs_tile(n):
                p, i = divmod(n, NTILE)
                stage_wait(act, n)
                if n == 2 * NTILE:
                    all_quantised(act, 0)
                if n % NTILE:
                    act.wait_ge(abs_done, p // 2 * NTILE + i)
                nc.scalar.activation(wint[:, 0, :].bitcast(BF16), stage_tile(n), ACT.Abs,
                                     accum_out=wsum[:, p // 2, i:i + 1]).then_inc(abs_done, 1)

            act.wait_ge(consts_made, 4)
            root(tiny[:, 3, 0:1], ones[0:S, 0:1])
            ln1_sums(1)
            ln1_sums(3)
            ln1_root(0)
            copy_unit(0, "K", 0)
            copy_unit(0, "K", 1)
            ln1_sums(5)
            for m in range(4):
                copy_xn(m)
            split_hi(0)
            for m in range(4, KC):
                copy_xn(m)
            ln1_sums(7)
            ln1_root(1)
            copy_unit(0, "Q", 0)
            for m in range(KC, 2 * KC):
                copy_xn(m)
            split_hi(1)
            copy_unit(0, "Q", 1)
            act.wait_ge(g_in, 32)
            nc.scalar.activation(gt[:], gates[:], ACT.Tanh).then_inc(gate_done, 1)
            for s in range(NGROUP + 3):
                if s < NGROUP:
                    act.wait_ge(max_done, s + 1)
                    if s >= NSM:
                        act.wait_ge(p_turned, s - NSM + 1)
                    if s >= 2:
                        act.wait_ge(rcp_done, s - 1)
                    for b in range(HB):
                        last = nc.scalar.activation(sm[:, s % NSM, b, :], bank[3 + s % 2][0:S, b * S:(b + 1) * S],
                                                    ACT.Exp, bias=smax[:, s % 2, b:b + 1],
                                                    accum_out=ssum[:, s % 2, b:b + 1])
                    last.then_inc(exp_done, 1)
                for t in tiles_rounded(s - 1):
                    if not by_dve(t):
                        sign_tile(t)
                for unit in slot_units.get(s, []):
                    if unit[1] in "KQ":
                        copy_unit(*unit)
                if 2 <= s < NGROUP + 2:
                    g = s - 2
                    act.wait_ge(p_turned, g + 1)
                    if g >= 2:
                        act.wait_ge(pv_done, g - 1)
                    nc.scalar.copy(pT[:, g % 2, :], bank[5 + g % 2][0:S, 0:HALF]).then_inc(pT_out, 1)
                if 4 <= s < NGROUP + 3 and s % 2 == 0:
                    q = (s - 4) // 2
                    act.wait_ge(pv_done, 2 * q + 2)
                    if q == 0:
                        act.wait_ge(v_ws, 1)
                    nc.scalar.activation(attn_T[:, 0, q // 2, (q % 2) * HALF:(q % 2 + 1) * HALF], bank[7][:, 0:HALF],
                                         ACT.Copy, scale=ws[:, NJOB:NJOB + 1]).then_inc(attn_out, 1)
                if s - 2 in job_slot:
                    split_hi(job_slot[s - 2])
                for n in tiles_of.get(s, []):
                    if n // NTILE % 2 == 0:
                        abs_tile(n)

            def centre(n):
                act.wait_ge(mean_done, n + 1)
                if n == 0:
                    act.wait_ge(pv_done, NGROUP)
                if n == HB:
                    act.wait_ge(xi_done, HB)
                for t in range(2):
                    ins = nc.scalar.activation(xc_rows[:, n % HB, t * 512:(t + 1) * 512],
                                               bank[3 + 2 * (n % 2) + t][0:S, :], ACT.Identity,
                                               bias=tiny[:, 7, n:n + 1])
                ins.then_inc(xc_done, 1)

            def round_x(n):
                act.wait_ge(k_done, n // HB + 1)
                if n >= 2:
                    act.wait_ge(xb_done, n - 1)
                nc.scalar.activation(xi_rows[:, n % 2, :], xc_rows[:, n % HB, :], ACT.Copy,
                                     scale=tiny[:, 5, n:n + 1]).then_inc(xi_done, 1)

            def copy_xq(n):
                act.wait_ge(xq_turned, n + 1)
                src = bank[7 - n % 2][:, 0:KC * S // 2].bitcast(BF16).rearrange("p (c t) -> p c t", c=KC)
                nc.scalar.copy(xq_T[:, :, n * S:(n + 1) * S], src).then_inc(xq_out, 1)

            def copy_d(half):
                act.wait_ge(d_done, half + 1)
                nc.scalar.copy(d_bc[:, half, :], bank[3][:, 0:HALF]).then_inc(d_out, 1)

            def gelu(half, j):
                q = half * FC + j
                act.wait_ge(f1_scaled, q + 1)
                if q >= HSLOTS + HG:
                    act.wait_ge(h_int, q - HSLOTS - HG + 1)
                elif q == HSLOTS:
                    act.wait_ge(w_int, 2 * NTILE)
                elif q == 0:
                    act.wait_ge(o_done, 2 * KC)
                nc.scalar.activation(h_slots(q)[:, 0], bank[q % 3][:, 0:HALF], ACT.Gelu).then_inc(h_done, 1)

            def round_h(q):
                act.wait_ge(h_mul, q + 1)
                if q == 0:
                    all_quantised(act, 1)
                if q >= 2:
                    act.wait_ge(hq_done, q - 1)
                nc.scalar.copy(hint[:, q % 2, :], h_slots(q)[:, 0]).then_inc(h_int, 1)

            def copy_s(half):
                act.wait_ge(se_done, half + 1)
                if half == 0:
                    act.wait_ge(w_int, 2 * NTILE)
                else:
                    act.wait_ge(h_mul, FC)
                nc.scalar.copy(s_bc, bank[3][:, 0:HALF])
                nc.scalar.copy(e_bc[:, half, :], bank[4][:, 0:HALF]).then_inc(s_out, 1)

            ln2 = {"centre": centre, "round": round_x, "xq": copy_xq, "d": copy_d}
            for s in range(NGROUP + 3, FFN_SLOT - 3):
                for n in tiles_of.get(s, []):
                    abs_tile(n)
                if 39 <= s < 39 + HB:
                    centre(s - 39)
            for n in range(HB):
                round_x(n)
            for n in range(HB):
                copy_xq(n)
            copy_d(0)
            for j in range(FC):
                gelu(0, j)
                for step, n in AT_BLOCK_ACT.get(j, []):
                    ln2[step](n)
                for t in tiles_rounded(FFN_SLOT + j - 2):
                    if not by_dve(t):
                        sign_tile(t)
            for j in range(FC):
                if j >= LAG:
                    round_h(j - LAG)
                gelu(1, j)
                if j == 5:
                    copy_s(0)
            for j in range(FC - LAG, FC):
                round_h(j)
            copy_s(1)
            for j in range(FC):
                round_h(FC + j)

        @block.vector
        def _(dve):
            count = [0]

            def link(ins):
                count[0] += 1
                ins.then_inc(dve_own, 1)
                dve.wait_ge(dve_own, count[0])

            def inv_root(hs):
                ve, r, t = (tiny[:, i, hs] for i in (0, 2, 3))
                link(nc.vector.tensor_tensor(t, r, r, ALU.mult))
                link(nc.vector.tensor_tensor(t, t, ve, ALU.mult))
                link(nc.vector.tensor_scalar(t, t, -0.5, 1.5, ALU.mult, ALU.add))
                link(nc.vector.tensor_tensor(r, r, t, ALU.mult))

            def largest(job):
                raw, _, arrived, value = job_data(job)
                dve.wait_ge(arrived, value)
                nc.vector.tensor_reduce(wm[:, job:job + 1], raw, AX.X, ALU.max, apply_absolute_value=True)\
                    .then_inc(wm_done, 1)

            def power_below(v):
                link(nc.vector.tensor_scalar(v, v, TINY, None, ALU.max))
                link(nc.vector.tensor_scalar(v.bitcast(I32), v.bitcast(I32), EXPONENT, None, ALU.bitwise_and))

            def scale(job):
                dve.wait_ge(wg_done, AT[job] + 1)
                g = wg[:, job:job + 1]
                power_below(g)
                link(nc.vector.reciprocal(ws[:, job:job + 1], g))
                if job < KC:
                    nc.vector.tensor_scalar(wi[:, job:job + 1], g, HD ** -0.5 / (TOP * XN_SCALE), None, ALU.mult)
                else:
                    if job == KC:
                        dve.wait_ge(gate_done, 1)
                    link(nc.vector.tensor_scalar(wi[:, job:job + 1], g, 1.0 / TOP, wi[:, NJOB:NJOB + 1],
                                                 ALU.mult, ALU.mult))
                    nc.vector.tensor_tensor(wi[:, job:job + 1], wi[:, job:job + 1], gt[:, 0:1], ALU.mult)
                nc.vector.tensor_scalar(ws[:, job:job + 1], ws[:, job:job + 1], TOP, None, ALU.mult)\
                    .then_inc(ws_done, 1)

            def split_lo(job):
                raw, pair, _, _ = job_data(job)
                dve.wait_ge(w_hi, AT[job] + 1)
                nc.vector.scalar_tensor_tensor(pair[:, 1], raw, ws[:, job:job + 1], pair[:, 0],
                                               ALU.mult, ALU.subtract).then_inc(w_lo, 1)

            def v_magnitudes():
                dve.wait_ge(ctx_in, 16)
                dve.wait_ge(wv_in, 16)
                nc.vector.tensor_reduce(wm[:, NJOB:NJOB + 1], region_c[:], AX.X, ALU.max, apply_absolute_value=True)
                nc.vector.tensor_reduce(wm[:, NJOB + 1:NJOB + 2], wv_all, AX.X, ALU.max, apply_absolute_value=True)\
                    .then_inc(v_wm, 1)

            def attn_scale():
                dve.wait_ge(v_wg, 1)
                g = wg[:, NJOB:NJOB + 1]
                link(nc.vector.scalar_tensor_tensor(g, g, float(L), wg[:, NJOB + 1:NJOB + 2], ALU.mult, ALU.mult))
                power_below(g)
                link(nc.vector.reciprocal(ws[:, NJOB:NJOB + 1], g))
                nc.vector.tensor_scalar(wi[:, NJOB:NJOB + 1], g, 1.0 / TOP, None, ALU.mult)
                nc.vector.tensor_scalar(ws[:, NJOB:NJOB + 1], ws[:, NJOB:NJOB + 1], TOP, None, ALU.mult)\
                    .then_inc(v_ws, 1)

            def ln1_stats(b):
                dve.wait_ge(x_in[b], 16)
                for t in range(2):
                    last = nc.vector.bn_stats(bn[:, b, t, :], x_rows[:, b, t * 512:(t + 1) * 512])
                link(last)
                link(nc.vector.bn_aggr(mv[:, b, :], bn[:, b, :, :]))

            def ln1_norm(half):
                hs = slice(half * HB, (half + 1) * HB)
                even, odd = (slice(half * HB + i, (half + 1) * HB, 2) for i in range(2))
                nc.vector.tensor_scalar(tiny[:, 7, even], mv[:, even, 0], -1.0, None, ALU.mult)
                nc.vector.tensor_scalar(tiny[:, 0, even], mv[:, even, 1], LN_EPS, None, ALU.add)
                dve.wait_ge(ln1_act, HB // 2 * (half + 1))
                nc.vector.tensor_scalar(tiny[:, 0, odd], sums[:, 1, odd], 1.0 / H, LN_EPS, ALU.mult, ALU.add)\
                    .then_inc(ln1_var, 1)
                dve.wait_ge(ln1_sd, half + 1)
                link(nc.vector.reciprocal(tiny[:, 2, hs], tiny[:, 1, hs]))
                inv_root(hs)
                link(nc.vector.tensor_scalar(tiny[:, 2, hs], tiny[:, 2, hs], XN_SCALE, None, ALU.mult))
                nc.vector.tensor_tensor(tiny[:, 6, hs], tiny[:, 7, hs], tiny[:, 2, hs], ALU.mult).then_inc(ln1_ready, 1)
                for b in range(half * HB, (half + 1) * HB, 2):
                    nc.vector.tensor_scalar(x_rows[:, b, :], x_rows[:, b, :], tiny[:, 7, b:b + 1], tiny[:, 2, b:b + 1],
                                            ALU.add, ALU.mult).then_inc(x_normed, 1)

            def xn_low(m):
                half, c = divmod(m, KC)
                t = slice(half * HALF, (half + 1) * HALF)
                dve.wait_ge(xn_hi, m + 1)
                nc.vector.tensor_tensor(xn_T[:, 1, c, t], bank[3 + m % 5][:, 0:HALF], xn_T[:, 0, c, t], ALU.subtract)\
                    .then_inc(xn_lo, 1)

            def copy_v(c, half):
                u = NUMBER[c, "V", half]
                projected(dve, (c, "V", half))
                if c >= 2:
                    dve.wait_ge(pv_done, 4 * (c - 1))
                nc.vector.tensor_copy(v_rows[:, c % 2, half * HB:(half + 1) * HB, :],
                                      bank[u % 3][0:S, :].rearrange("p (b f) -> p b f", b=HB)).then_inc(v_out, 1)

            def clip_tile(t):
                dve.wait_ge(w_int, t + 1)
                nc.vector.tensor_scalar(quantised_tile(t), wint[:, t % NWI, :].rearrange("p (k m) -> p k m", k=KC),
                                        1.0, -1.0, ALU.min, ALU.max, saturate=False).then_inc(w_quant, 1)

            def sum_columns(w):
                dve.wait_ge(abs_done, NTILE * (w + 1))
                nc.vector.tensor_reduce(wtot[:, w, 0:1], wsum[:, w, :], AX.X, ALU.add).then_inc(sums_done, 1)

            def finish_scale(w):
                if w == 0:
                    projected(dve, SUM_W1)
                else:
                    dve.wait_ge(tot_done, 1)
                src = bank[NUMBER[SUM_W1] % 3 if w == 0 else 5]
                link(nc.vector.tensor_scalar(wtot[:, w, 1:2], src[:, 0:1], 1.0 / (F * H), Q_EPS,
                                             ALU.mult, ALU.max))
                link(nc.vector.reciprocal(wtot[:, w, 2:3], wtot[:, w, 1:2]))
                nc.vector.tensor_scalar(wtot[:, w, 3:4], wtot[:, w, 1:2], 1.0 / Q_MAX, None, ALU.mult)\
                    .then_inc(scale_done, 1)

            ln1_stats(0)
            ln1_stats(2)
            largest(0)
            ln1_norm(0)
            ln1_stats(4)
            scale(0)
            for m in range(3):
                xn_low(m)
            ln1_stats(6)
            for m in range(3, KC):
                xn_low(m)
            split_lo(0)
            copy_v(0, 0)
            copy_v(0, 1)
            ln1_norm(1)
            largest(1)
            for m in range(KC, 2 * KC):
                xn_low(m)
            scale(1)
            split_lo(1)

            def attn_low(q):
                dve.wait_ge(attn_out, q + 1)
                c, t = q // 2, slice(q % 2 * HALF, (q % 2 + 1) * HALF)
                nc.vector.scalar_tensor_tensor(attn_T[:, 1, c, t], bank[7][:, 0:HALF], ws[:, NJOB:NJOB + 1],
                                               attn_T[:, 0, c, t], ALU.mult, ALU.subtract).then_inc(attn_lo, 1)

            def invert_sums(g):
                dve.wait_ge(exp_done, g + 1)
                if g >= 2:
                    dve.wait_ge(normed, g - 1)
                nc.vector.reciprocal(srcp[:, g % 2, :], ssum[:, g % 2, :]).then_inc(rcp_done, 1)

            for s in range(NGROUP):
                if s:
                    invert_sums(s - 1)
                dve.wait_ge(scores_done, s + 1)
                link(nc.vector.tensor_reduce(smax[:, s % 2, :],
                                             bank[3 + s % 2][0:S, 0:HALF].rearrange("p (b k) -> p b k", b=HB),
                                             AX.X, ALU.max))
                nc.vector.tensor_scalar(smax[:, s % 2, :], smax[:, s % 2, :], -1.0, None, ALU.mult)\
                    .then_inc(max_done, 1)
                for t in tiles_rounded(s - 1):
                    if by_dve(t):
                        clip_tile(t)
                if s >= 5 and s % 2 == 1:
                    attn_low((s - 5) // 2)
                if s == MEAN_SLOT + 1:
                    finish_scale(0)
                for c, kind, half in slot_units.get(s, []):
                    if kind == "V":
                        copy_v(c, half)
                if s == 0:
                    v_magnitudes()
                if s == 2:
                    attn_scale()
                if s in job_slot:
                    largest(job_slot[s])
                if s - 1 in job_slot:
                    scale(job_slot[s - 1])
                if s - 3 in job_slot:
                    split_lo(job_slot[s - 3])
                if s == MEAN_SLOT - 1:
                    sum_columns(0)
            invert_sums(NGROUP - 1)

            def gated_add(u):
                half, o = divmod(u, KC)
                dve.wait_ge(o_done, u + 1)
                if u < KC and u % 2 == 0:
                    dve.wait_ge(xT_in[u // 2], 16)
                x2 = x2_T[:, o, half * HALF:(half + 1) * HALF]
                nc.vector.scalar_tensor_tensor(x2, bank[u % 3][:, 0:HALF], wi[:, KC + o:KC + o + 1], x2,
                                               ALU.mult, ALU.add)\
                    .then_inc(x2_out, 1)

            def ln2_stats(n):
                dve.wait_ge(x2_turned, n + 1)
                for t in range(2):
                    last = nc.vector.bn_stats(bn[:, n, t, :], bank[3 + 2 * (n % 2) + t][0:S, :])
                link(last)
                link(nc.vector.bn_aggr(mv[:, n, :], bn[:, n, :, :]))
                nc.vector.tensor_scalar(tiny[:, 7, n:n + 1], mv[:, n, 0:1], -1.0, None, ALU.mult).then_inc(mean_done, 1)

            def ln2_absmax(n):
                dve.wait_ge(xc_done, n + 1)
                link(nc.vector.tensor_reduce(tiny[:, 4, n:n + 1], xc_rows[:, n % HB, :], AX.X, ALU.max,
                                             apply_absolute_value=True))

            def ln2_var_step(half):
                hs = slice(half * HB, (half + 1) * HB)
                nc.vector.tensor_scalar(tiny[:, 0, hs], mv[:, hs, 1], LN_EPS, None, ALU.add).then_inc(ln2_var, 1)

            def ln2_scales(half):
                hs = slice(half * HB, (half + 1) * HB)
                dve.wait_ge(ln2_root, half + 1)
                inv_root(hs)
                r, t, am, k, d = (tiny[:, i, hs] for i in (2, 3, 4, 5, 6))
                link(nc.vector.tensor_tensor(am, am, r, ALU.mult))
                link(nc.vector.tensor_scalar(am, am, Q_EPS, None, ALU.max))
                link(nc.vector.reciprocal(t, am))
                nc.vector.scalar_tensor_tensor(k, t, Q_MAX, r, ALU.mult, ALU.mult).then_inc(k_done, 1)
                link(nc.vector.tensor_scalar(d, am, wtot[0:S, 0, 3:4], None, ALU.mult))
                if half:
                    dve.wait_ge(d_done, 1)
                spread(0, d).then_inc(d_diag, 1)

            def spread(r, v):
                return nc.vector.tensor_tensor(diag[:, r, :].rearrange("p (b k) -> p b k", b=HB),
                                               ident[0:S, 0:S].unsqueeze(1).to_broadcast([S, HB, S]),
                                               v.to_broadcast([S, HB, S]), ALU.mult)

            def cast_x(n):
                dve.wait_ge(xi_done, n + 1)
                if n >= 2:
                    dve.wait_ge(xq_turned, n - 1)
                nc.vector.tensor_copy(xb_rows[:, n % 2, :], xi_rows[:, n % 2, :]).then_inc(xb_done, 1)

            ln2 = {"stats": ln2_stats, "absmax": ln2_absmax, "var": ln2_var_step, "scales": ln2_scales,
                   "cast": cast_x, "sum": sum_columns}
            attn_low(2 * KC - 2)
            for u in range(2 * KC):
                if u == 3:
                    attn_low(2 * KC - 1)
                if u == 13:
                    cast_x(0)
                    cast_x(1)
                if u == 14:
                    cast_x(2)
                    cast_x(3)
                if u == 15:
                    finish_scale(1)
                gated_add(u)
                for step, n in AT_OUTPUT_DVE.get(u, []):
                    ln2[step](n)
            def scale_block(q):
                dve.wait_ge(f1_done, q + 1)
                if q % FC == 0:
                    dve.wait_ge(d_out, q // FC + 1)
                nc.vector.tensor_tensor(bank[q % 3][:, 0:HALF], bank[q % 3][:, 0:HALF], d_bc[:, q // FC, :], ALU.mult)\
                    .then_inc(f1_scaled, 1)

            def run_max(g):
                dve.wait_ge(h_done, HG * (g + 1))
                h = h_slots(HG * g, HG).rearrange("p j t -> p t j")
                if g % (FC // HG) == 0:
                    if g:
                        dve.wait_ge(run_turned, 1)
                    nc.vector.tensor_reduce(run, h, AX.X, ALU.max, apply_absolute_value=True).then_inc(run_done, 1)
                else:
                    link(nc.vector.tensor_reduce(run4[:], h, AX.X, ALU.max, apply_absolute_value=True))
                    dve.wait_ge(run_done, g)
                    nc.vector.tensor_tensor(run, run, run4[:], ALU.max).then_inc(run_done, 1)

            def cast_h(q):
                dve.wait_ge(h_int, q + 1)
                half, j = divmod(q, FC)
                if q == 0:
                    dve.wait_ge(xq_turned, B)
                if q == FC:
                    dve.wait_ge(f1_done, 2 * FC)
                nc.vector.tensor_copy(hq[half][:, j, :], hint[:, q % 2, :]).then_inc(hq_done, 1)

            def h_scales(half):
                dve.wait_ge(run_turned, half + 1)
                am, s, e = (tiny[:, i, 0:HB] for i in (4, 5, 6))
                link(nc.vector.tensor_reduce(am, bank[3][0:S, :].rearrange("p (b f) -> p b f", b=HB), AX.X, ALU.max))
                link(nc.vector.tensor_scalar(am, am, Q_EPS, None, ALU.max))
                link(nc.vector.reciprocal(s, am))
                link(nc.vector.tensor_scalar(s, s, Q_MAX, None, ALU.mult))
                link(nc.vector.tensor_scalar(e, am, wtot[0:S, 1, 3:4], gt[0:S, 1:2], ALU.mult, ALU.mult))
                dve.wait_ge(d_done, 2)
                if half:
                    dve.wait_ge(se_done, 1)
                spread(0, s).then_inc(se_diag, 1)
                spread(1, e).then_inc(se_diag, 1)

            for q in range(2 * FC):
                scale_block(q)
                if q > FC + LAG:
                    cast_h(q - FC - LAG - 1)
                if q % HG == 0 and q:
                    run_max(q // HG - 1)
                for step, n in AT_BLOCK_DVE.get(q, []):
                    ln2[step](n)
                for t in tiles_rounded(FFN_SLOT + q - 2):
                    if by_dve(t):
                        clip_tile(t)
                if q == FC + 3:
                    h_scales(0)
            run_max(2 * FC // HG - 1)
            for j in range(FC - LAG - 1, FC):
                cast_h(j)
            h_scales(1)
            for u in range(2 * KC):
                if u < KC:
                    for j in range(4 * u - 4, 4 * u) if u < KC - 1 else range(4 * u - 4, FC):
                        if j >= 0:
                            cast_h(FC + j)
                half, o = divmod(u, KC)
                dve.wait_ge(f2_done, u + 1)
                dve.wait_ge(s_out, half + 1)
                if u >= 2:
                    dve.wait_ge(y_out[u % 2], 16 * (u // 2))
                y = y_sb[:, u % 2, :]
                nc.vector.tensor_tensor(y, bank[(2 * FC + u) % 3][:, 0:HALF], e_bc[:, half, :], ALU.mult)\
                    .then_inc(y_scaled, 1)
                dve.wait_ge(y_scaled, u + 1)
                nc.vector.tensor_tensor(y, y, x2_T[:, o, half * HALF:(half + 1) * HALF], ALU.add).then_inc(y_added, 1)

        @block.tensor
        def _(pe):
            def turn_x(half):
                pe.wait_ge(consts_made, 4)
                pe.wait_ge(x_normed, HB // 2 * (half + 1))
                pe.wait_ge(x_normed_pool, HB // 2 * (half + 1))
                for c in range(KC):
                    m = half * KC + c
                    if m >= 5:
                        pe.wait_ge(xn_lo, m - 4)
                    for b in range(HB):
                        last = nc.tensor.transpose(bank[3 + m % 5][:, b * S:(b + 1) * S],
                                                   x_rows[:, half * HB + b, c * P:(c + 1) * P], ident[0:S, 0:S])
                    last.then_inc(tr1_done, 1)

            def split_product(out, w, x, ks, first, final):
                for k in ks:
                    wk = [w[:, p, k * P:(k + 1) * P] for p in range(2)]
                    xk = [x[:, p, k] for p in range(2)]
                    for n, (a, b) in enumerate(((0, 0), (0, 1), (1, 0))):
                        last = nc.tensor.matmul(out, wk[a], xk[b], start=(k == first and n == 0),
                                                stop=(k == final and n == 2))
                return last

            def project(c, kind, half, ks=range(KC)):
                u = NUMBER[c, kind, half]
                if u >= 3 and 0 in ks:
                    unit_copied(pe, unit_order[u - 3])
                w = wkv_sb[:, c % 2]
                t = slice(half * HALF, (half + 1) * HALF)
                if kind in "KV":
                    pe.wait_ge(wkv_in[c % 2], 16 * (c // 2 + 1))
                    if c == 0:
                        pe.wait_ge(ctx_in, 16)
                if kind == "S":
                    last = total(0)
                elif kind == "K":
                    for k in range(LC):
                        last = nc.tensor.matmul(bank[u % 3][:, 0:HALF], w[:, k, :], ctx_sb[:, k, t],
                                                start=(k == 0), stop=(k == LC - 1))
                elif kind == "V":
                    for b in range(HB):
                        n = half * HB + b
                        for k in range(LC):
                            last = nc.tensor.matmul(bank[u % 3][0:S, b * P:(b + 1) * P],
                                                    ctx_sb[:, k, n * S:(n + 1) * S], w[:, LC + k, :],
                                                    start=(k == 0), stop=(k == LC - 1))
                else:
                    pe.wait_ge(w_lo, AT[c] + 1)
                    if c == 0:
                        pe.wait_ge(xn_lo, KC * (half + 1))
                    last = split_product(bank[u % 3][:, 0:HALF], wq_p[:, c % 2], xn_T[:, :, :, t], ks, 0, KC - 1)
                if KC - 1 in ks:
                    last.then_inc(proj_done, 1)

            def scores(g):
                c, half, h = g // 4, g // 2 % 2, g % 2
                unit_copied(pe, (c, "Q", half))
                unit_copied(pe, (c, "K", half))
                if g == 0:
                    pe.wait_ge(xn_lo, 2 * KC)
                if g >= 2:
                    pe.wait_ge(exp_done, g - 1)
                rows = slice(HD * h, HD * (h + 1))
                for b in range(HB):
                    t = slice((half * HB + b) * S, (half * HB + b + 1) * S)
                    out = bank[3 + g % 2][0:S, b * S:(b + 1) * S]
                    nc.tensor.matmul(out, ident_b[0:S, 0:S], mask[:], start=True, stop=False)
                    last = nc.tensor.matmul(out, q_T[rows, c % 2, t], k_T[rows, c % 2, t], start=False, stop=True)
                last.then_inc(scores_done, 1)

            def turn_p(g):
                pe.wait_ge(normed, g + 1)
                if g >= 2:
                    pe.wait_ge(pT_out, g - 1)
                for b in range(HB):
                    last = nc.tensor.transpose(bank[5 + g % 2][0:S, b * S:(b + 1) * S], sm[:, g % NSM, b, :],
                                               ident[0:S, 0:S])
                last.then_inc(p_turned, 1)

            def weigh_v(g):
                c, half, h = g // 4, g // 2 % 2, g % 2
                pe.wait_ge(pT_out, g + 1)
                unit_copied(pe, (c, "V", half))
                if h == 0 and g:
                    pe.wait_ge(attn_lo, g // 2)
                for b in range(HB):
                    last = nc.tensor.matmul(bank[7][HD * h:HD * (h + 1), b * S:(b + 1) * S],
                                            v_rows[:, c % 2, half * HB + b, HD * h:HD * (h + 1)],
                                            pT[:, g % 2, b * S:(b + 1) * S], start=True, stop=True)
                last.then_inc(pv_done, 1)

            def total(w):
                pe.wait_ge(sums_done, w + 1)
                out = bank[NUMBER[SUM_W1] % 3 if w == 0 else 5]
                return nc.tensor.matmul(out[:, 0:1], ones[:], wtot[:, w, 0:1], start=True, stop=True)

            def out_proj(u, ks=range(KC)):
                half, o = divmod(u, KC)
                if 0 in ks:
                    pe.wait_ge(w_lo, NJOB)
                    if u < 3:
                        pe.wait_ge(v_out, 2 * KC)
                        pe.wait_ge(qk_out, 4 * KC)
                    else:
                        pe.wait_ge(x2_out, u - 2)
                pe.wait_ge(attn_lo, 2 * ks[-1] + 1 + half)
                last = split_product(bank[u % 3][:, 0:HALF], wout_p[:, :, o],
                                     attn_T[:, :, :, half * HALF:(half + 1) * HALF], ks, 0, KC - 1)
                if KC - 1 in ks:
                    last.then_inc(o_done, 1)

            def turn_x2(n):
                pe.wait_ge(x2_out, KC * (n // HB + 1))
                if n < 2:
                    pe.wait_ge((exp_done, pT_out)[n], NGROUP)
                else:
                    pe.wait_ge(xc_done, n - 1)
                if n == HB:
                    pe.wait_ge(d_out, 1)
                if n == HB + 1:
                    pe.wait_ge(scale_done, 2)
                for c in range(KC):
                    last = nc.tensor.transpose(bank[3 + 2 * (n % 2) + c // 4][0:S, c % 4 * P:(c % 4 + 1) * P],
                                               x2_T[:, c, n * S:(n + 1) * S], ident[:])
                last.then_inc(x2_turned, 1)

            def turn_xq(n):
                pe.wait_ge(xb_done, n + 1)
                if n == 0:
                    pe.wait_ge(attn_lo, 2 * KC)
                if n >= 2:
                    pe.wait_ge(xq_out, n - 1)
                out = bank[7 - n % 2][:, 0:KC * S // 2].bitcast(BF16)
                for c in range(KC):
                    last = nc.tensor.transpose(out[:, c * S:(c + 1) * S], xb_rows[:, n % 2, c * P:(c + 1) * P],
                                               ident_b[0:S, 0:S])
                last.then_inc(xq_turned, 1)

            def spread_d(half):
                pe.wait_ge(d_diag, half + 1)
                pe.wait_ge(xc_done, HB * (half + 1) - 1)
                nc.tensor.matmul(bank[3][:, 0:HALF], ones[0:S, :], diag[:, 0, :], start=True, stop=True)\
                    .then_inc(d_done, 1)

            def hidden(q):
                half, j = divmod(q, FC)
                if q < 3:
                    pe.wait_ge(x2_out, 2 * KC)
                else:
                    pe.wait_ge(h_done, q - 2)
                if q == 0:
                    all_quantised(pe, 0)
                if j == 0:
                    pe.wait_ge(xq_out, HB * (half + 1))
                for k in range(KC):
                    last = nc.tensor.matmul(bank[q % 3][:, 0:HALF], w1_q[:, j, k, :],
                                            xq_T[:, k, half * HALF:(half + 1) * HALF],
                                            start=(k == 0), stop=(k == KC - 1))
                last.then_inc(f1_done, 1)

            def turn_run(half):
                pe.wait_ge(run_done, FC // HG * (half + 1))
                pe.wait_ge((d_out, s_out)[half], 2 - half)
                for b in range(HB):
                    last = nc.tensor.transpose(bank[3][0:S, b * P:(b + 1) * P], run[:, b * S:(b + 1) * S], ident[:])
                last.then_inc(run_turned, 1)

            def spread_se(half):
                pe.wait_ge(se_diag, 2 * half + 2)
                nc.tensor.matmul(bank[3][:, 0:HALF], ones[0:S, :], diag[:, 0, :], start=True, stop=True)
                nc.tensor.matmul(bank[4][:, 0:HALF], ones[0:S, :], diag[:, 1, :], start=True, stop=True)\
                    .then_inc(se_done, 1)

            def output(u):
                half, o = divmod(u, KC)
                q = 2 * FC + u
                if u < 3:
                    pe.wait_ge(h_done, q - 2)
                else:
                    pe.wait_ge(y_scaled, u - 2)
                if u == 0:
                    all_quantised(pe, 1)
                for k in range(FC):
                    if o == 0:
                        pe.wait_ge(hq_done, FC * half + k + 1)
                    last = nc.tensor.matmul(bank[q % 3][:, 0:HALF], w2_q[:, o, k, :], hq[half][:, k, :],
                                            start=(k == 0), stop=(k == FC - 1))
                    if u == 1 and k == KC:
                        spread_se(1)
                last.then_inc(f2_done, 1)

            project(0, "K", 0)
            project(0, "K", 1)
            turn_x(0)
            project(0, "V", 0)
            project(0, "V", 1)
            project(0, "Q", 0)
            turn_x(1)
            project(0, "Q", 1)
            for s in range(NGROUP + 3):
                if s < NGROUP:
                    scores(s)
                for unit in slot_units.get(s, []):
                    project(*unit, part_of_q.get((s, unit), range(KC)))
                for (at, unit), ks in part_of_q.items():
                    if at == s and KC - 1 not in ks:
                        project(*unit, ks)
                if s in HEAD_START:
                    out_proj(HEAD_START[s], range(KC - 1))
                if 2 <= s < NGROUP + 2:
                    turn_p(s - 2)
                if s == NGROUP + 2:
                    out_proj(4)
                if s >= 3:
                    weigh_v(s - 3)
                if s == NGROUP + 1:
                    for u in range(3):
                        out_proj(u, range(KC - 1, KC))
                    out_proj(3)
            for u in range(5, 2 * KC):
                out_proj(u)
                for n in {8: (0, 1), 9: (2,), 10: (3,)}.get(u, ()):
                    turn_x2(n)
                for n in {14: (0, 1), 15: (2, 3)}.get(u, ()):
                    turn_xq(n)
                if u == 14:
                    pe.wait_ge(xc_done, HB)
                    total(1).then_inc(tot_done, 1)
            spread_d(0)
            for q in range(2 * FC):
                hidden(q)
                for step, n in AT_BLOCK_PE.get(q, []):
                    (turn_x2 if step == "x2" else turn_xq if step == "xq" else spread_d)(n)
                if q == FC + 2:
                    turn_run(0)
                if q == FC + 5:
                    spread_se(0)
            for u in range(2 * KC):
                output(u)
                if u == 0:
                    turn_run(1)


def kernel(x, ctx_512, g_xattn, g_ffn, L0_xattn_Wq, L0_xattn_Wkv_expand, L0_xattn_Wout, L0_ffn_w1, L0_ffn_w2):
    import numpy as np
    import concourse.bacc as bacc
    from concourse.bass_utils import run_bass_kernel_spmd

    def a(v):
        return np.asarray(v)

    x, ctxs = a(x), a(ctx_512)

    def tiles(w):
        o, i = w.shape
        return w.reshape(o // P, P, i // P, P).transpose(0, 3, 2, 1)

    wkv = a(L0_xattn_Wkv_expand)
    arrays = {
        "x_tok": x,
        "x_t": x.reshape(N, KC, P).transpose(2, 1, 0),
        "ctx_t": ctxs[:, :S].reshape(N, LC, P).transpose(2, 1, 0),
        "wq": tiles(a(L0_xattn_Wq)).reshape(KC, P, H),
        "wkv": np.concatenate([tiles(wkv[:H]), tiles(wkv[H:])], axis=2),
        "wv": tiles(wkv[H:]).transpose(1, 0, 2, 3).reshape(P, LC * H),
        "wout": tiles(a(L0_xattn_Wout)).reshape(KC, P, H),
        "w1": tiles(a(L0_ffn_w1)),
        "w2": tiles(a(L0_ffn_w2)).reshape(KC, P, 4, KC * P).transpose(0, 2, 1, 3),
        "g_attn": np.broadcast_to(a(g_xattn).reshape(1, 1), (P, 1)),
        "g_ffn": np.broadcast_to(a(g_ffn).reshape(1, 1), (P, 1)),
    }
    arrays["w1"] = arrays["w1"].reshape(FC, P, H)
    arrays["w2"] = arrays["w2"].reshape(FC, P, H)
    arrays = {k: np.ascontiguousarray(v) for k, v in arrays.items()}
    nc = bacc.Bacc("TRN2", target_bir_lowering=False, num_devices=1, dynamic_dma_scratch_size=1024)
    aps = [nc.dram_tensor(k, v.shape, mybir.dt.from_np(v.dtype), kind="ExternalInput").ap() for k, v in arrays.items()]
    out = nc.dram_tensor("out_t", (KC, P, N), F32, kind="ExternalOutput").ap()
    flamingo_layer(nc, *aps, out)
    r = run_bass_kernel_spmd(nc, [arrays], core_ids=[0])
    got = r.results[0]["out_t"]
    return np.ascontiguousarray(got.reshape(H, N).T).reshape(B, S, H)
```
